# Optimizing a Trainium2 kernel written in Bass

```python
import numpy as np
import jax
import jax.numpy as jnp

def _softmax(x, axis=-1):
    return jax.nn.softmax(x, axis=axis)
def _gelu(x):
    return jax.nn.gelu(x, approximate=True)
def _silu(x):
    return jax.nn.silu(x)
def _sigmoid(x):
    return jax.nn.sigmoid(x)
def _layernorm(x, axis=-1, eps=1e-5):
    m = jnp.mean(x, axis=axis, keepdims=True)
    v = jnp.var(x, axis=axis, keepdims=True)
    return (x - m) / jnp.sqrt(v + eps)
def _scatter_add(tgt, idx, src, axis=0):
    return tgt.at[idx].add(src)
def _segment_sum(src, seg, n):
    return jax.ops.segment_sum(src, seg, n)

kernel_name = 'mk_adj_resnorm_d4_adj_64_e7ca5b'

def setup_inputs(seed: int = 0):
    np.random.seed(seed)
    _w = jnp.asarray
    def _rec_inputs():
        import jax
        import jax.numpy as jnp
        _gk = jax.random.key(seed)
        x = -0.000929 + 1 * jax.random.normal(jax.random.fold_in(_gk, 1), (8192, 64), jnp.float32)
        _a = jax.random.bernoulli(jax.random.fold_in(_gk, 2), 0.00195312, (8192, 8192))
        _a = jnp.logical_or(_a, jnp.eye(8192, dtype=bool))
        _af = _a.astype(jnp.float32)
        _af = _af * jax.random.uniform(jax.random.fold_in(_gk, 3), (8192, 8192), jnp.float32, 0.05, 1)
        adj = _af
        return x, adj
    x, adj = _rec_inputs()
    def _L0_gnn_setup():
        import jax, jax.numpy as jnp
        import numpy as np
        N, D, H = (16384, 64, 256)
        GAIN = 0.2
        key = jax.random.key(seed)
        ks = jax.random.split(key, 6)
        X = jax.random.normal(ks[0], (N, D), dtype=jnp.float32)
        t = jax.random.uniform(ks[1], (1,), dtype=jnp.float32)
        Wt = jax.random.uniform(ks[2], (N, N), dtype=jnp.float32)
        B = GAIN * jnp.eye(D, dtype=jnp.float32) + 0.01 * jax.random.normal(ks[3], (D, D), dtype=jnp.float32)
        W1 = jax.random.normal(ks[4], (D + 1, H), dtype=jnp.float32) * (1.0 / np.sqrt(D + 1))
        b1 = jnp.zeros((H,), dtype=jnp.float32)
        W2 = jax.random.normal(ks[5], (H, D), dtype=jnp.float32) * (1.0 / np.sqrt(H))
        b2 = jnp.zeros((D,), dtype=jnp.float32)
        return {'X': X, 't': t, 'Wt': Wt, 'B': B, 'W1': W1, 'b1': b1, 'W2': W2, 'b2': b2}
    _L0_gnn_all = _L0_gnn_setup()
    _L0_gnn_in = {k: v for k, v in _L0_gnn_all.items() if k in ('t', 'B', 'W1', 'b1', 'W2', 'b2', )}
    del _L0_gnn_all

    def _L1_gnn_setup():
        import jax, jax.numpy as jnp
        import numpy as np
        N, F_IN, F_OUT, K = (16384, 64, 64, 3)
        key = jax.random.key(seed)
        k1, k2, k3, k4 = jax.random.split(key, 4)
        x = jax.random.normal(k1, (N, F_IN), dtype=jnp.float32)
        L_tilde = jax.random.normal(k2, (N, N), dtype=jnp.float32) / np.float32(np.sqrt(N))
        stdv = 1.0 / np.sqrt(F_OUT)
        weights = jax.random.uniform(k3, (K + 1, F_IN, F_OUT), dtype=jnp.float32, minval=-stdv, maxval=stdv)
        bias = jax.random.uniform(k4, (F_OUT,), dtype=jnp.float32, minval=-stdv, maxval=stdv)
        return {'x': x, 'L_tilde': L_tilde, 'weights': weights, 'bias': bias}
    _L1_gnn_all = _L1_gnn_setup()
    _L1_gnn_in = {k: v for k, v in _L1_gnn_all.items() if k in ('weights', 'bias', )}
    del _L1_gnn_all

    def _L2_gnn_setup():
        import jax, jax.numpy as jnp
        import numpy as np
        N, D_IN, D_OUT = (16384, 64, 64)
        AVG_DEG = 32.0
        L2_EPS = 1e-12
        key = jax.random.key(seed)
        kx, ka, kw, kb = jax.random.split(key, 4)
        X = jax.random.normal(kx, (N, D_IN), dtype=jnp.float32)
        adj = (jax.random.uniform(ka, (N, N)) < AVG_DEG / N).astype(jnp.float32)
        bound = 1.0 / np.sqrt(2 * D_IN)
        W = jax.random.uniform(kw, (2 * D_IN, D_OUT), dtype=jnp.float32, minval=-bound, maxval=bound)
        b = jax.random.uniform(kb, (D_OUT,), dtype=jnp.float32, minval=-bound, maxval=bound)
        return {'X': X, 'adj': adj, 'W': W, 'b': b}
    _L2_gnn_all = _L2_gnn_setup()
    _L2_gnn_in = {k: v for k, v in _L2_gnn_all.items() if k in ('W', 'b', )}
    del _L2_gnn_all

    def _L3_gnn_setup():
        import jax, jax.numpy as jnp
        import numpy as np
        N, D_IN, D_OUT = (8192, 64, 64)
        MAX_NEIGH = 100
        DECAY = 0.5
        key = jax.random.key(seed)
        k1, k2, k3, k4 = jax.random.split(key, 4)
        stdv = 1.0 / np.sqrt(D_OUT)
        inputs = {'input': jax.random.normal(k1, (N, D_IN), dtype=jnp.float32), 'adj': jax.random.randint(k2, (N, N), 0, 2).astype(jnp.float32), 'weight': jax.random.uniform(k3, (D_IN, D_OUT), minval=-stdv, maxval=stdv, dtype=jnp.float32), 'bias': jax.random.uniform(k4, (D_OUT,), minval=-stdv, maxval=stdv, dtype=jnp.float32)}
        return inputs
    _L3_gnn_all = _L3_gnn_setup()
    _L3_gnn_in = {k: v for k, v in _L3_gnn_all.items() if k in ('weight', 'bias', )}
    del _L3_gnn_all

    return {
        "x": x,
        "adj": adj,
        "L0_gnn_t": _L0_gnn_in["t"],
        "L0_gnn_B": _L0_gnn_in["B"],
        "L0_gnn_W1": _L0_gnn_in["W1"],
        "L0_gnn_b1": _L0_gnn_in["b1"],
        "L0_gnn_W2": _L0_gnn_in["W2"],
        "L0_gnn_b2": _L0_gnn_in["b2"],
        "L1_gnn_weights": _L1_gnn_in["weights"],
        "L1_gnn_bias": _L1_gnn_in["bias"],
        "L2_gnn_W": _L2_gnn_in["W"],
        "L2_gnn_b": _L2_gnn_in["b"],
        "L3_gnn_weight": _L3_gnn_in["weight"],
        "L3_gnn_bias": _L3_gnn_in["bias"],
    }

def reference(x, adj, L0_gnn_t, L0_gnn_B, L0_gnn_W1, L0_gnn_b1, L0_gnn_W2, L0_gnn_b2, L1_gnn_weights, L1_gnn_bias, L2_gnn_W, L2_gnn_b, L3_gnn_weight, L3_gnn_bias):
    import jax
    import jax.numpy as jnp
    def _L0_gnn_ref(X, t, Wt, B, W1, b1, W2, b2):
        import jax, jax.numpy as jnp
        import numpy as np
        N, D, H = (16384, 64, 256)
        GAIN = 0.2
        n = X.shape[0]
        tcol = jnp.broadcast_to(t.reshape(1, 1), (n, 1))
        h = jnp.tanh(jnp.concatenate([X, tcol], axis=1) @ W1 + b1)
        u_intra = h @ W2 + b2
        XB = X @ B.T
        u_comm = Wt @ XB - jnp.sum(Wt, axis=1, keepdims=True) * XB
        return u_intra + u_comm

    def _L1_gnn_ref(x, L_tilde, weights, bias):
        import jax, jax.numpy as jnp
        import numpy as np
        N, F_IN, F_OUT, K = (16384, 64, 64, 3)
        T_prev = x
        out = T_prev @ weights[0]
        T_curr = L_tilde @ x
        out = out + T_curr @ weights[1]
        for k in range(2, K + 1):
            T_next = 2.0 * (L_tilde @ T_curr) - T_prev
            out = out + T_next @ weights[k]
            T_prev, T_curr = (T_curr, T_next)
        return out + bias

    def _L2_gnn_ref(X, adj, W, b):
        import jax, jax.numpy as jnp
        import numpy as np
        N, D_IN, D_OUT = (16384, 64, 64)
        AVG_DEG = 32.0
        L2_EPS = 1e-12
        deg = jnp.clip(jnp.sum(adj, axis=1, keepdims=True) + 1.0, 1.0, None)
        h_neigh = (adj @ X + X) / deg
        concat = jnp.concatenate([X, h_neigh], axis=1)
        z = concat @ W + b
        out = jax.nn.relu(z)
        norm = jnp.linalg.norm(out, axis=1, keepdims=True)
        return out / jnp.maximum(norm, L2_EPS)

    def _L3_gnn_ref(input, adj, weight, bias):
        import jax, jax.numpy as jnp
        import numpy as np
        N, D_IN, D_OUT = (8192, 64, 64)
        MAX_NEIGH = 100
        DECAY = 0.5
        support = input @ weight
        mask = (adj != 0).astype(support.dtype)
        rank = jnp.cumsum(mask, axis=1)
        deg = rank[:, -1:]
        k = jnp.minimum(deg, float(MAX_NEIGH))
        pos = rank - (deg - k)
        w = mask * jnp.where(pos > 0, DECAY ** (k - pos), 0.0)
        out = w @ support + bias
        return out

    x = _layernorm(x + _L0_gnn_ref(x, L0_gnn_t, adj, L0_gnn_B, L0_gnn_W1, L0_gnn_b1, L0_gnn_W2, L0_gnn_b2), axis=-1)
    x = _layernorm(x + _L1_gnn_ref(x, adj, L1_gnn_weights, L1_gnn_bias), axis=-1)
    x = _layernorm(x + _L2_gnn_ref(x, adj, L2_gnn_W, L2_gnn_b), axis=-1)
    x = _layernorm(x + _L3_gnn_ref(x, adj, L3_gnn_weight, L3_gnn_bias), axis=-1)
    return x


_drawn_inputs = setup_inputs


def setup_inputs(seed=0):
    import zlib

    import numpy as np

    out = dict(_drawn_inputs(seed))
    spreads = {'L0_gnn_b1': (0.0, 0.1), 'L0_gnn_b2': (0.0, 0.1)}
    factors = {'L1_gnn_bias': 64.0, 'L2_gnn_b': 5.873}
    for name, (base, spread) in spreads.items():
        noise = np.random.default_rng([zlib.crc32(name.encode()), seed]).standard_normal(out[name].shape)
        drawn = base * np.exp(spread * noise) if base else spread * noise
        out[name] = jnp.asarray(drawn.astype(out[name].dtype))
    for name, factor in factors.items():
        out[name] = (out[name] * factor).astype(out[name].dtype)
    return out
```

```python
import concourse.bass as bass
from concourse import mybir
from concourse.alu_op_type import AluOpType as ALU


def spend(eng, sem, n=1):
    eng.sem_inc(sem, -n)


def graph_layers(nc, at, x_rows, x_cols, t_col, b_t, w1, w1_t, b1_c, w2, bias_rows, l1_w, l2_w, l3_w,
                 ident, rank_mats, out):
    f32, f32r, bf16, u16 = mybir.dt.float32, mybir.dt.float32r, mybir.dt.bfloat16, mybir.dt.uint16
    ACT = mybir.ActivationFunctionType
    AX = mybir.AxisListType.X

    P = 128
    D = x_cols.shape[0]
    N = x_cols.shape[1]
    BLK = 1024
    NB = N // BLK
    G = N // P
    Q = BLK // P
    NQ = 4
    SUB = Q // NQ
    RING = 4
    HALF = 512
    HID = w1.shape[1]
    HC = HID // P
    EPS = 1e-5
    L2_EPS = 1e-12
    CUT = 100
    MARK = 127
    SCALE = float(2 ** (127 - CUT))

    at_off = [nc.sbuf_base]

    def place(name, shape, dt, at_byte=None):
        size = 4 if dt in (f32, f32r) else 2
        for n in shape[1:]:
            size *= n
        off = (at_off[0] + 31) // 32 * 32 if at_byte is None else at_byte
        if at_byte is None:
            at_off[0] = off + size
        return nc.alloc_sbuf_tensor_at(name, shape, dt, offset=off), off

    T, T_at = place("T", [P, 2, G, P], f32r)
    SV, SV_at = place("SV", [P, N], f32)
    O, _ = place("O", [P, G, D], f32)
    raw, raw_at = place("raw", [P, NQ, SUB, BLK], f32)
    hi, hi_at = place("hi", [P, RING, BLK], f32r)
    lo, lo_at = place("lo", [P, RING, BLK], f32r)
    st, _ = place("st", [P, NQ, 2, SUB, P], f32r)
    UT, _ = place("UT", [P, BLK], f32)
    TT, _ = place("TT", [D, BLK], f32)
    xr, _ = place("xr", [P, Q, D], f32)
    sq, _ = place("sq", [P, Q, D], f32)
    xo, _ = place("xo", [P, Q, D], f32)
    eye, _ = place("eye", [P, P], f32)
    pick1, _ = place("pick1", [P, D + 1], f32)
    comb, _ = place("comb", [P, 2 * D], f32)
    comb4, _ = place("comb4", [P, D], f32)
    w02, _ = place("w02", [D, D], f32)
    l2w_sb, _ = place("l2w_sb", [D, 2 * D], f32)
    l3w_sb, _ = place("l3w_sb", [D, D], f32)
    ones_st, _ = place("ones_st", [P, P], f32r)
    zst, _ = place("zst", [P, P], bf16)
    zmv, _ = place("zmv", [P, HALF], bf16)
    rank_b, _ = place("rank_b", [P, 2, P], bf16)
    bias, _ = place("bias", [P, 4, D], f32)
    RS, _ = place("RS", [P, G], f32)
    RD, _ = place("RD", [P, G], f32)
    st1, _ = place("st1", [P, Q], f32)
    st2, _ = place("st2", [P, Q], f32)
    st3, _ = place("st3", [P, Q], f32)
    relu_bias, _ = place("relu_bias", [P, 1], f32)
    hT, _ = place("hT", [P, HC, BLK], f32, hi_at)
    w1_sb, _ = place("w1_sb", [D, HID], f32, lo_at)
    w2_sb, _ = place("w2_sb", [P, HC, D], f32, lo_at + 4 * HID)
    bt_sb, _ = place("bt_sb", [D, D], f32, lo_at + 4 * HID + 4 * HC * D)
    hb_sb, _ = place("hb_sb", [P, 3, HC], f32, lo_at + 4 * HID + 4 * HC * D + 4 * D)
    l1w_sb, _ = place("l1w_sb", [P, 4, D], f32, lo_at + 8192)
    rank_f, _ = place("rank_f", [P, 2, P], f32, hi_at + 4 * HC * BLK)
    S_ov, _ = place("S_ov", [P, 2, G, 2 * P], bf16, T_at)
    S, _ = place("S", [P, G, 3 * D], bf16, SV_at)
    M, _ = place("M", [P, 4, BLK], bf16, hi_at)
    Wt, _ = place("Wt", [P, 2, BLK], u16, lo_at)
    assert at_off[0] <= nc.sbuf_usable_end, at_off

    sem = nc.alloc_semaphore

    raw_ready = [sem(f"raw_ready{k}") for k in range(NQ)]
    raw_free = [sem(f"raw_free{k}") for k in range(NQ)]
    hi_ready = [sem(f"hi_ready{b}") for b in range(RING)]
    hi_free = [sem(f"hi_free{b}") for b in range(RING)]
    lo_done = sem("lo_done")
    lo_ready = [sem(f"lo_ready{b}") for b in range(RING)]
    lo_free = [sem(f"lo_free{b}") for b in range(RING)]
    st_ready = [sem(f"st_ready{k}") for k in range(NQ)]
    st_free = [sem(f"st_free{k}") for k in range(NQ)]
    b_done, b_free = sem("b_done"), sem("b_free")
    a_done, a_free = sem("a_done"), sem("a_free")
    evac_done = sem("evac_done")
    ut_ready = sem("ut_ready")
    fin_ready = sem("fin_ready")
    fin2_ready = sem("fin2_ready")
    xo_ready, xr_pe = sem("xo_ready"), sem("xr_pe")
    v_ready = sem("v_ready")
    tp_ready = sem("tp_ready")
    tt_ready = sem("tt_ready")
    var_ready, sd_ready = sem("var_ready"), sem("sd_ready")
    dve_chain, pool_chain = sem("dve_chain"), sem("pool_chain")
    c_hid, c_x, c_rest = sem("c_hid"), sem("c_x"), sem("c_rest")
    c_hid2, c_rest2 = sem("c_hid2"), sem("c_rest2")
    h_ready, tanh_ready = sem("h_ready"), sem("tanh_ready")
    hb_ready = sem("hb_ready")
    pre_fin, pre_free = sem("pre_fin"), sem("pre_free")
    const_ready = sem("const_ready")
    pool_const = sem("pool_const")
    pre_done = sem("pre_done")
    s_copied = sem("s_copied")
    m_ready = [sem(f"m_ready{k}") for k in range(2)]
    m_free = [sem(f"m_free{k}") for k in range(4)]
    r_ready = [sem(f"r_ready{k}") for k in range(2)]
    w_ready = [sem(f"w_ready{k}") for k in range(2)]
    w_free = [sem(f"w_free{k}") for k in range(2)]
    o_done, o_free = sem("o_done"), sem("o_free")
    out_ready, out_free, out_all = sem("out_ready"), sem("out_free"), sem("out_all")

    PSAB = nc.alloc_psum_tensor("PSAB", [P, 4, HALF], f32)
    PSA = PSAB[:, 0:2, :].rearrange("p h n -> p (h n)")
    PSB = PSAB[:, 2:4, :].rearrange("p h n -> p (h n)")
    PSF = nc.alloc_psum_tensor("PSF", [P, Q, P], f32)
    PST = nc.alloc_psum_tensor("PST", [P, BLK], f32)[:]
    PSF_flat = PSF[:].rearrange("p q n -> p (q n)")

    def ph(slot):
        return slice(D * slot, D * slot + D)

    def u_slot(k):
        return (k - 1) % 2

    def block_of(k, r):
        return r if k % 2 else NB - 1 - r

    def sweep_rows(eng, k, row):
        row(k, 0, None if k == 1 else (k - 1, block_of(k - 1, NB - 1)), k == 1, False)
        last = NB - 1 if k == 1 else NB
        if last > 1:
            with eng.Fori(1, last) as r:
                row(k, r, (k, block_of(k, r - 1)), k == 1, True)
        if k == 1:
            row(k, NB - 1, (k, block_of(k, NB - 2)), False, True)

    def units(eng, k, r, upper, unit):
        if upper:
            with eng.Fori(r + 1, NB) as J:
                unit(J)
        else:
            with eng.Fori(0, r) as o:
                unit(o if k % 2 else NB - 1 - o)

    with nc.Block() as block:

        @block.sync
        def _(sp):
            for dst, src in ((w1_sb, w1), (w2_sb, w2), (bt_sb, b_t)):
                sp.dma_start(dst[:], src).then_inc(c_hid, 16)
            for n, src in enumerate((w1_t, b1_c, t_col)):
                sp.dma_start(hb_sb[:, n, :], src).then_inc(c_hid2, 16)
            sp.dma_start(SV[0:D, :], x_cols).then_inc(c_x, 16)
            sp.dma_start(O[:], x_rows).then_inc(c_rest, 16)
            sp.dma_start(bias[:], bias_rows).then_inc(c_rest, 16)
            for lo_p in (0, D):
                sp.dma_start(l1w_sb[lo_p:lo_p + D], l1_w).then_inc(c_rest, 16)
            sp.dma_start(eye[:], ident).then_inc(c_rest, 16)
            sp.dma_start(l2w_sb[:], l2_w).then_inc(c_rest2, 16)
            sp.dma_start(l3w_sb[:], l3_w).then_inc(c_rest2, 16)
            sp.dma_start(rank_f[:], rank_mats).then_inc(c_rest2, 16)
            for k in range(NQ):
                sp.sem_inc(raw_free[k], 1)

            def load(I, J, quarters=range(NQ)):
                for k, q in enumerate(quarters):
                    sp.wait_ge(raw_free[k], 1)
                    spend(sp, raw_free[k])
                    sp.dma_start(raw[:, k], at[bass.ds((I * NB + J) * NQ + q, 1)].rearrange(
                        "o p (s i) -> (o p) s i", s=SUB)).then_inc(raw_ready[k], 16)

            def row(k, r, prev, upper, off):
                I = block_of(k, r)
                load(I, I)
                if upper:
                    units(sp, k, r, True, lambda J: load(I, J))
                if off:
                    units(sp, k, r, False, lambda J: load(I, J))

            for k in range(1, 6):
                sweep_rows(sp, k, row)
            with sp.Fori(0, NB) as I:
                with sp.Fori(0, NB) as o:
                    load(I, NB - 1 - o, range(NQ - 1, -1, -1))

        @block.gpsimd
        def _(pool):
            def link(ins):
                ins.then_inc(pool_chain, 1)
                pool.wait_ge(pool_chain, 1)
                spend(pool, pool_chain)

            nc.gpsimd.memset(T[:, 0, :, ph(1)].bitcast(f32), 1.0)
            nc.gpsimd.memset(T[:, 1, :, ph(1)].bitcast(f32), 0.0)
            nc.gpsimd.memset(ones_st[:, ph(0)].bitcast(f32), 0.0)
            nc.gpsimd.memset(ones_st[:, ph(1)].bitcast(f32), 1.0)
            nc.gpsimd.memset(zst[:], 0.0)
            nc.gpsimd.memset(zmv[:], 0.0)
            link(nc.gpsimd.memset(pick1[:], 0.0))
            link(nc.gpsimd.memset(pick1[D:D + 1, D:D + 1], 1.0))
            pool.sem_inc(pool_const, 1)

        @block.scalar
        def _(act):
            for b in range(RING):
                act.sem_inc(hi_free[b], 1)
            for q in range(NQ - 1):
                act.sem_inc(st_free[q], 1)
            act.wait_ge(c_x, 16)
            act.wait_ge(hb_ready, 1)
            spend(act, hb_ready)
            with act.Fori(0, NB) as I:
                for c in range(HC):
                    act.wait_ge(h_ready, 1)
                    spend(act, h_ready)
                    nc.scalar.activation(hT[:, c, :], (PSA, PSB)[c], ACT.Tanh,
                                         bias=hb_sb[:, 0, c:c + 1]).then_inc(tanh_ready, 1)
                nc.scalar.copy(TT[:], SV[0:D, bass.ds(I * BLK, BLK)]).then_inc(tt_ready, 1)
            act.wait_ge(pre_done, 1)
            spend(act, pre_done)
            act.wait_ge(pool_const, 1)

            def prepare(k, J, quarters=range(NQ)):
                for q in quarters:
                    split_hi(q)
                    operand(k, J, q)

            def split_hi(q):
                act.wait_ge(raw_ready[q], 16)
                spend(act, raw_ready[q], 16)
                for s in range(SUB):
                    b = (q * SUB + s) % RING
                    act.wait_ge(hi_free[b], 1)
                    spend(act, hi_free[b])
                    nc.scalar.copy(hi[:, b], raw[:, q, s]).then_inc(hi_ready[b], 1)

            def operand(k, J, q):
                act.wait_ge(st_free[q], 1)
                spend(act, st_free[q])
                g = bass.ds(J * Q + q * SUB, SUB)
                if k == 5:
                    src, dst = T[:, :, g, ph(0)], st[:, q, :, :, ph(0)]
                else:
                    src, dst = T[:, :, g, :], st[:, q]
                nc.scalar.copy(dst, src.bitcast(f32)).then_inc(st_ready[q], 1)

            def evacuate(k, I):
                u, v = ph(u_slot(k)), ph(1 - u_slot(k))
                cols = bass.ds(I * BLK, BLK)
                if k == 1:
                    act.wait_ge(b_done, 1)
                    spend(act, b_done)
                    nc.scalar.copy(UT[:], PSB).then_inc(b_free, 1)
                    nc.scalar.copy(SV[v, cols], PSA[v, :]).then_inc(evac_done, 1)
                else:
                    act.wait_ge(a_done, 1)
                    spend(act, a_done)
                    nc.scalar.copy(UT[u, :], PSA[u, :]).then_inc(evac_done, 1)
                    if k < 5:
                        nc.scalar.copy(SV[v, cols], PSA[v, :]).then_inc(a_free, 1)

            def transposed(k, stage):
                if (k, stage) in ((5, 0), (5, 2), (1, 2)):
                    act.wait_ge(tp_ready, 1)
                    spend(act, tp_ready)
                    nc.scalar.copy(TT[:], PST[0:D, :]).then_inc(tt_ready, 1)

            def roots(k):
                for _ in range({1: 1, 2: 0, 3: 0, 4: 1, 5: 2}[k]):
                    act.wait_ge(var_ready, 1)
                    spend(act, var_ready)
                    nc.scalar.activation(st2[:], st1[:], ACT.Sqrt).then_inc(sd_ready, 1)

            def row(k, r, prev, upper, off):
                I = block_of(k, r)
                if prev and prev[0] != k:
                    split_hi(0)
                    split_hi(1)
                    transposed(prev[0], 0)
                    evacuate(*prev)
                    roots(prev[0])
                    transposed(prev[0], 2)
                    act.wait_ge(v_ready, 1)
                    spend(act, v_ready)
                    operand(k, I, 0)
                    operand(k, I, 1)
                else:
                    prepare(k, I, (0, 1))
                    if prev:
                        transposed(k, 0)
                        evacuate(*prev)
                prepare(k, I, (2, 3))
                if prev and prev[0] == k:
                    roots(k)
                if upper:
                    units(act, k, r, True, lambda J: prepare(k, J))
                if prev and prev[0] == k and k < 5:
                    act.wait_ge(v_ready, 1)
                    spend(act, v_ready)
                if off:
                    units(act, k, r, False, lambda J: prepare(k, J))
                if prev and prev[0] == k:
                    transposed(k, 2)

            for k in range(1, 6):
                sweep_rows(act, k, row)
            transposed(5, 0)
            evacuate(5, block_of(5, NB - 1))
            roots(5)
            transposed(5, 2)

            for b in range(2):
                act.sem_inc(w_free[b], 1)
            with act.Fori(0, NB) as I:
                with act.Fori(0, NB) as o:
                    for n in range(Q):
                        b = n % 2
                        act.wait_ge(r_ready[b], 1)
                        spend(act, r_ready[b])
                        act.wait_ge(w_free[b], 1)
                        spend(act, w_free[b])
                        nc.scalar.activation(Wt[:, b, :], (PSF_flat, PST)[b], ACT.Relu, scale=-128.0,
                                             bias=relu_bias[:, 0:1]).then_inc(w_ready[b], 1)
                act.wait_ge(var_ready, 1)
                spend(act, var_ready)
                nc.scalar.activation(st2[:], st1[:], ACT.Sqrt).then_inc(sd_ready, 1)
                act.wait_ge(out_ready, 1)
                spend(act, out_ready)
                act.dma_start(out[bass.ds(I, 1)].rearrange("o p q d -> (o p) q d"), xr[:]).then_inc(out_all, 16)
                act.wait_ge(out_all, 16)
                act.sem_inc(out_all, -16)
                act.sem_inc(out_free, 1)

        @block.vector
        def _(dve):
            def link(ins):
                ins.then_inc(dve_chain, 1)
                dve.wait_ge(dve_chain, 1)
                spend(dve, dve_chain)

            def rows(col):
                return col.unsqueeze(2).broadcast_to([P, Q, D])

            def feats(row):
                return row.unsqueeze(1).broadcast_to([P, Q, D])

            for b in range(RING):
                dve.sem_inc(lo_free[b], 1)
            tt, ts = nc.vector.tensor_tensor, nc.vector.tensor_scalar
            stt, copy = nc.vector.scalar_tensor_tensor, nc.vector.tensor_copy

            dve.wait_ge(c_hid2, 48)
            link(tt(hb_sb[:, 0, :], hb_sb[:, 0, :], hb_sb[:, 2, :], ALU.mult))
            tt(hb_sb[:, 0, :], hb_sb[:, 0, :], hb_sb[:, 1, :], ALU.add).then_inc(hb_ready, 1)
            dve.wait_ge(c_rest, 80)
            dve.wait_ge(c_rest2, 48)
            with dve.Fori(0, NB) as I:
                g = bass.ds(I * Q, Q)
                th, tl = T[:, 0, g, ph(0)], T[:, 1, g, ph(0)]
                dve.wait_ge(pre_fin, 1)
                spend(dve, pre_fin)
                link(copy(th, PSF[:, :, 0:D]))
                link(tt(O[:, g, :], O[:, g, :], PSF[:, :, D:2 * D], ALU.add))
                link(tt(O[:, g, :], O[:, g, :], feats(bias[:, 0, :]), ALU.add))
                tt(tl, PSF[:, :, 0:D], th.bitcast(f32), ALU.subtract).then_inc(pre_free, 1)
            a0, a1 = ph(0), ph(1)
            copy(rank_b[:], rank_f[:])
            tt(w02[:], l1w_sb[a0, 0, :], l1w_sb[a0, 2, :], ALU.subtract)
            copy(comb[a1, 0:D], eye[a1, D:2 * D])
            tt(comb[a1, D:2 * D], l1w_sb[a1, 1, :], l1w_sb[a1, 3, :], ALU.subtract).then_inc(pre_done, 1)
            ts(comb[a0, 0:D], eye[a0, 0:D], 2.0, None, ALU.mult)
            ts(comb[a0, D:2 * D], l1w_sb[a0, 2, :], 2.0, None, ALU.mult)
            ts(comb4[a1, :], l1w_sb[a1, 3, :], 2.0, None, ALU.mult)
            nc.vector.memset(relu_bias[:], float(128 * (CUT - MARK)))
            dve.wait_ge(pool_const, 1)
            copy(pick1[a0, 0:D], eye[a0, 0:D]).then_inc(const_ready, 1)

            def split_lo(quarters):
                for q in quarters:
                    for s in range(SUB):
                        b = (q * SUB + s) % RING
                        dve.wait_ge(hi_ready[b], 1)
                        spend(dve, hi_ready[b])
                        dve.wait_ge(lo_free[b], 1)
                        spend(dve, lo_free[b])
                        ins = tt(lo[:, b], raw[:, q, s], hi[:, b].bitcast(f32), ALU.subtract)
                        if s < SUB - 1:
                            ins.then_inc(lo_ready[b], 1)
                        else:
                            ins.then_inc(lo_done, 1)
                    dve.wait_ge(lo_done, 1)
                    spend(dve, lo_done)
                    dve.sem_inc(lo_ready[b], 1)
                    dve.sem_inc(raw_free[q], 1)

            def add_partial(k, I):
                u = ph(u_slot(k))
                dve.wait_ge(evac_done, 1)
                spend(dve, evac_done)
                if k == 1:
                    tt(UT[u, :], UT[u, :], PSA[u, :], ALU.add).then_inc(ut_ready, 1)
                else:
                    tt(UT[u, :], UT[u, :], SV[u, bass.ds(I * BLK, BLK)], ALU.add).then_inc(ut_ready, 1)

            def add_diagonal(k, I):
                if k > 1:
                    u, cols = ph(u_slot(k)), bass.ds(I * BLK, BLK)
                    dve.wait_ge(b_done, 1)
                    spend(dve, b_done)
                    tt(SV[u, cols], SV[u, cols], PSB[u, :], ALU.add).then_inc(b_free, 1)

            def normalise(dst, signal):
                link(nc.vector.tensor_reduce(st1[:], xr[:], AX, ALU.add))
                link(stt(xr[:], rows(st1[:]), -1.0 / D, xr[:], ALU.mult, ALU.add))
                link(tt(sq[:], xr[:], xr[:], ALU.mult))
                link(nc.vector.tensor_reduce(st1[:], sq[:], AX, ALU.add))
                ts(st1[:], st1[:], 1.0 / D, EPS, ALU.mult, ALU.add).then_inc(var_ready, 1)
                dve.wait_ge(sd_ready, 1)
                spend(dve, sd_ready)
                link(nc.vector.reciprocal(st3[:], st2[:]))
                tt(dst, xr[:], rows(st3[:]), ALU.mult).then_inc(signal, 1)

            def whole(k, I):
                if k % 2:
                    src = T[:, :, bass.ds(I * Q, Q), ph(1 if k == 3 else 0)].bitcast(f32)
                    ins = tt(xo[:], src[:, 0], src[:, 1], ALU.add)
                    if k == 5:
                        ins.then_inc(xo_ready, 1)
                    else:
                        link(ins)

            def write_v(k, I):
                dst = T[:, :, bass.ds(I * Q, Q), ph(1 - u_slot(k))]
                link(copy(dst[:, 0], xr[:]))
                tt(dst[:, 1], xr[:], dst[:, 0].bitcast(f32), ALU.subtract).then_inc(v_ready, 1)

            def finish(k, I):
                g = bass.ds(I * Q, Q)
                f0, f1 = PSF[:, :, 0:D], PSF[:, :, D:2 * D]
                dve.wait_ge(fin_ready, 1)
                spend(dve, fin_ready)
                if k == 1:
                    link(copy(RS[:, g], PSF[:, :, D]))
                    link(tt(sq[:], xo[:], rows(RS[:, g]), ALU.mult))
                    link(tt(xr[:], f0, sq[:], ALU.subtract))
                    link(tt(xr[:], xr[:], O[:, g, :], ALU.add))
                    normalise(xr[:], dve_chain)
                    dve.wait_ge(dve_chain, 1)
                    spend(dve, dve_chain)
                    dve.sem_inc(xr_pe, 1)
                    write_v(k, I)
                elif k == 2:
                    link(copy(xr[:], f0))
                    write_v(k, I)
                    tt(O[:, g, :], O[:, g, :], f1, ALU.add)
                elif k == 3:
                    link(tt(xr[:], f0, xo[:], ALU.subtract))
                    write_v(k, I)
                    tt(O[:, g, :], O[:, g, :], f1, ALU.add)
                elif k == 4:
                    link(tt(xr[:], f0, O[:, g, :], ALU.add))
                    normalise(xr[:], dve_chain)
                    dve.wait_ge(dve_chain, 1)
                    spend(dve, dve_chain)
                    write_v(k, I)
                else:
                    link(tt(sq[:], f1, rows(RD[:, g]), ALU.mult))
                    link(tt(xr[:], f0, sq[:], ALU.add))
                    link(tt(xr[:], xr[:], feats(bias[:, 2, :]), ALU.add))
                    link(stt(sq[:], xr[:], 0.0, xr[:], ALU.max, ALU.mult))
                    nc.vector.tensor_reduce(st1[:], sq[:], AX, ALU.add).then_inc(var_ready, 1)
                    dve.wait_ge(sd_ready, 1)
                    spend(dve, sd_ready)
                    link(ts(st3[:], st2[:], L2_EPS, None, ALU.max))
                    link(nc.vector.reciprocal(st3[:], st3[:]))
                    link(stt(xr[:], xr[:], 0.0, rows(st3[:]), ALU.max, ALU.mult))
                    link(tt(xr[:], xr[:], xo[:], ALU.add))
                    normalise(xr[:], dve_chain)
                    dve.wait_ge(dve_chain, 1)
                    spend(dve, dve_chain)
                    copy(O[:, g, :], xr[:]).then_inc(xr_pe, 1)

            def after(k, I):
                g = bass.ds(I * Q, Q)
                if k == 1:
                    link(ts(RD[:, g], RS[:, g], 1.0, 1.0, ALU.add, ALU.max))
                    nc.vector.reciprocal(RD[:, g], RD[:, g])
                    dve.wait_ge(fin2_ready, 1)
                    spend(dve, fin2_ready)
                    link(tt(O[:, g, :], xr[:], PSF[:, :, 0:D], ALU.add))
                    link(tt(O[:, g, :], O[:, g, :], feats(bias[:, 1, :]), ALU.add))
                elif k == 5:
                    s1, s2, s3 = S_ov[:, 0, g, P:P + D], S_ov[:, 0, g, P + D:2 * P], S_ov[:, 1, g, P:P + D]
                    dve.wait_ge(fin2_ready, 1)
                    spend(dve, fin2_ready)
                    link(ts(sq[:], PSF[:, :, 0:D], SCALE, None, ALU.mult))
                    link(copy(s1, sq[:]))
                    link(tt(sq[:], sq[:], s1, ALU.subtract))
                    link(copy(s2, sq[:]))
                    link(tt(s3, sq[:], s2, ALU.subtract))

            def row(k, r, prev, upper, off):
                if prev:
                    whole(*prev)
                split_lo((0, 1))
                if prev:
                    add_partial(*prev)
                    if prev[0] != k:
                        finish(*prev)
                        after(*prev)
                split_lo((2, 3))
                if prev and prev[0] == k:
                    finish(*prev)
                add_diagonal(k, block_of(k, r))
                if upper:
                    units(dve, k, r, True, lambda J: split_lo(range(NQ)))
                if off:
                    units(dve, k, r, False, lambda J: split_lo(range(NQ)))
                if prev and prev[0] == k:
                    after(*prev)

            for k in range(1, 6):
                sweep_rows(dve, k, row)
            last = block_of(5, NB - 1)
            whole(5, last)
            add_partial(5, last)
            finish(5, last)
            after(5, last)

            copy(S[:, :, 0:2 * D], S_ov[:, 0, :, P:2 * P])
            copy(S[:, :, 2 * D:3 * D], S_ov[:, 1, :, P:P + D]).then_inc(s_copied, 1)
            dve.sem_inc(m_free[1], 1)
            dve.sem_inc(m_free[2], 1)
            dve.sem_inc(out_free, 1)
            with dve.Fori(0, NB) as I:
                g = bass.ds(I * Q, Q)
                link(nc.vector.memset(M[:, 0, :], 0.0))
                with dve.Fori(0, NB) as o:
                    for k in range(NQ):
                        dve.wait_ge(raw_ready[k], 16)
                        spend(dve, raw_ready[k], 16)
                        for n in (k * SUB, k * SUB + 1):
                            old, new = n % 4, (n + 1) % 4
                            dve.wait_ge(m_free[new], 1)
                            spend(dve, m_free[new])
                            stt(M[:, new, :], raw[:, k, SUB - 1 - n % 2, :], 0.0, M[:, old, :],
                                ALU.not_equal, ALU.add).then_inc(lo_done, 1)
                            dve.wait_ge(lo_done, 1)
                            spend(dve, lo_done)
                            dve.sem_inc(m_ready[n % 2], 1)
                        dve.sem_inc(raw_free[k], 1)
                dve.wait_ge(o_done, 1)
                spend(dve, o_done)
                dve.wait_ge(out_free, 1)
                spend(dve, out_free)
                link(nc.vector.tensor_reduce(
                    xr[:].rearrange("p (a b) d -> p a b d", b=2),
                    PSAB[:, :, 0:6 * D].rearrange("p a (b t d) -> p a b d t", b=2, t=3), AX, ALU.add))
                dve.sem_inc(o_free, 1)
                link(tt(xr[:], xr[:], feats(bias[:, 3, :]), ALU.add))
                link(tt(xr[:], xr[:], O[:, g, :], ALU.add))
                normalise(xr[:], out_ready)

        @block.tensor
        def _(pe):
            mm = nc.tensor.matmul

            def small(dst, lhs, rhs, **kw):
                for q in range(Q):
                    last = mm(dst[:, q, :], lhs[:, q * P:(q + 1) * P], rhs, start=True, stop=True)
                return last

            pe.sem_inc(pre_free, 1)
            pe.sem_inc(b_free, 1)
            pe.sem_inc(a_free, 1)
            pe.wait_ge(c_hid, 48)
            pe.wait_ge(c_x, 16)
            with pe.Fori(0, NB) as I:
                for c in range(HC):
                    for h in range(2):
                        last = mm((PSA, PSB)[c][:, h * HALF:(h + 1) * HALF], w1_sb[:, c * P:(c + 1) * P],
                                  SV[0:D, bass.ds(I * BLK + h * HALF, HALF)], start=True, stop=True)
                    last.then_inc(h_ready, 1)
                pe.wait_ge(tt_ready, 1)
                spend(pe, tt_ready)
                pe.wait_ge(tanh_ready, HC)
                spend(pe, tanh_ready, HC)
                pe.wait_ge(pre_free, 1)
                spend(pe, pre_free)
                small(PSF[:, :, 0:D], TT, bt_sb[:])
                for q in range(Q):
                    for c in range(HC):
                        last = mm(PSF[:, q, D:2 * D], hT[:, c, q * P:(q + 1) * P], w2_sb[:, c, :],
                                  start=c == 0, stop=c == HC - 1)
                last.then_inc(pre_fin, 1)
            pe.wait_ge(const_ready, 1)
            spend(pe, const_ready)
            pe.wait_ge(pool_const, 1)

            def multiply(bank, quarters=range(NQ), sums_bank=None, start=False, stop=False):
                for q in quarters:
                    pe.wait_ge(st_ready[q], 1)
                    spend(pe, st_ready[q])
                    for s in range(SUB):
                        b = (q * SUB + s) % RING
                        first, last = start and q + s == 0, stop and q == NQ - 1 and s == SUB - 1
                        w_hi, w_lo = st[:, q, 0, s, :], st[:, q, 1, s, :]
                        pe.wait_ge(lo_ready[b], 1)
                        spend(pe, lo_ready[b])
                        terms = [(bank, w_hi, lo)] + [(sums_bank, ones_st[:], lo)] * (sums_bank is not None)
                        n_lo = 2 * len(terms)
                        terms += [(bank, w_hi, hi), (bank, w_lo, hi)]
                        terms += [(sums_bank, ones_st[:], hi)] * (sums_bank is not None)
                        for n in range(2 * len(terms)):
                            dst, w, src = terms[n // 2]
                            cols = slice(n % 2 * HALF, (n % 2 + 1) * HALF)
                            ins = mm(dst[:, cols], w, src[:, b, cols], start=first and n < 2,
                                     stop=last and n >= 2 * len(terms) - 2)
                            if n == 0 and s == 0:
                                ins.then_inc(st_free[(q - 1) % NQ], 1)
                            elif n == n_lo - 1:
                                ins.then_inc(lo_free[b], 1)
                            elif n == 2 * len(terms) - 1:
                                ins.then_inc(hi_free[b], 1)

            def zeros(bank, start):
                for h in range(2):
                    last = mm(bank[:, h * HALF:(h + 1) * HALF], zst[:], zmv[:], start=start, stop=not start)
                return last

            def transpose(src):
                for q in range(Q):
                    last = mm(PST[0:D, q * P:(q + 1) * P], src[:, q, :], eye[:], start=True, stop=True)
                last.then_inc(tp_ready, 1)

            def end0(k):
                if k == 5:
                    pe.wait_ge(xo_ready, 1)
                    spend(pe, xo_ready)
                    transpose(xo)

            def end1(k):
                u = ph(u_slot(k))
                pe.wait_ge(ut_ready, 1)
                spend(pe, ut_ready)
                if k == 1:
                    last = small(PSF[:, :, 0:D + 1], UT, pick1[:])
                elif k < 4:
                    last = small(PSF, UT[u, :], comb[u, :])
                elif k == 4:
                    last = small(PSF[:, :, 0:D], UT[u, :], comb4[u, :])
                else:
                    pe.wait_ge(tt_ready, 1)
                    spend(pe, tt_ready)
                    for q in range(Q):
                        mm(PSF[:, q, :], TT[:, q * P:(q + 1) * P], l2w_sb[:], start=True, stop=False)
                        last = mm(PSF[:, q, D:2 * D], UT[u, q * P:(q + 1) * P], l2w_sb[:, D:2 * D],
                                  start=False, stop=True)
                last.then_inc(fin_ready, 1)

            def end2(k):
                if k in (1, 5):
                    pe.wait_ge(xr_pe, 1)
                    spend(pe, xr_pe)
                    transpose(xr)

            def end3(k):
                if k in (1, 5):
                    pe.wait_ge(tt_ready, 1)
                    spend(pe, tt_ready)
                    small(PSF[:, :, 0:D], TT, w02[:] if k == 1 else l3w_sb[:]).then_inc(fin2_ready, 1)

            def row(k, r, prev, upper, off):
                same = prev and prev[0] == k
                if prev:
                    end0(prev[0])
                if prev and not same:
                    end1(prev[0])
                    end2(prev[0])
                    end3(prev[0])
                pe.wait_ge(b_free, 1)
                spend(pe, b_free)
                multiply(PSB, (0, 1), start=True)
                if same:
                    end1(k)
                multiply(PSB, (2, 3), stop=k > 1)
                if k > 1:
                    mm(PST[:, 0:2], zst[:], zmv[:, 0:2], start=True, stop=True).then_inc(b_done, 1)
                if upper:
                    units(pe, k, r, True, lambda J: multiply(PSB))
                if same:
                    end2(k)
                if 2 <= k <= 4 or (k == 5 and not same):
                    pe.wait_ge(a_free, 1)
                    spend(pe, a_free)
                zeros(PSA, True)
                if off:
                    units(pe, k, r, False, lambda J: multiply(PSA, sums_bank=PSB if k == 1 else None))
                if same:
                    end3(k)
                last = zeros(PSA, False)
                if k == 1:
                    last = zeros(PSB, False)
                    last.then_inc(b_done, 1)
                else:
                    last.then_inc(a_done, 1)

            for k in range(1, 6):
                sweep_rows(pe, k, row)
            end0(5)
            end1(5)
            end2(5)
            end3(5)

            pe.wait_ge(s_copied, 1)
            spend(pe, s_copied)
            pe.sem_inc(o_free, 1)
            ranks = (PSF_flat, PST)

            def rank(n):
                b, old, new = n % 2, n % 4, (n + 1) % 4
                pe.wait_ge(m_ready[b], 1)
                spend(pe, m_ready[b])
                terms = [(0, new, h) for h in range(2)] + [(1, old, h) for h in range(2)]
                for i, (m, src, h) in enumerate(terms):
                    ins = mm(ranks[b][:, h * HALF:(h + 1) * HALF], rank_b[:, m, :],
                             M[:, src, h * HALF:(h + 1) * HALF], start=i < 2, stop=i >= 2)
                    if i == 0:
                        ins.then_inc(m_free[(n - 1) % 4], 1)
                    elif i == 3:
                        ins.then_inc(r_ready[b], 1)

            def weigh(n, J):
                b = n % 2
                pe.wait_ge(w_ready[b], 1)
                spend(pe, w_ready[b])
                g = J * Q + (Q - 1 - n)
                for q in range(Q):
                    last = mm(PSAB[:, q // 2, (q % 2) * 3 * D:(q % 2 + 1) * 3 * D],
                              Wt[:, b, q * P:(q + 1) * P].bitcast(bf16), S[:, bass.ds(g, 1), :].rearrange(
                                  "p o n -> p (o n)"), start=False, stop=False)
                last.then_inc(w_free[b], 1)

            def bounds(start):
                for a in range(4):
                    last = mm(PSAB[:, a, 0:6 * D], zst[:], zmv[:, 0:6 * D], start=start, stop=not start)
                return last

            with pe.Fori(0, NB) as I:
                pe.wait_ge(o_free, 1)
                spend(pe, o_free)
                bounds(True)
                with pe.Fori(0, NB) as o:
                    J = NB - 1 - o
                    rank(0)
                    for n in range(1, Q):
                        rank(n)
                        weigh(n - 1, J)
                    weigh(Q - 1, J)
                bounds(False).then_inc(o_done, 1)


_INS = ["at", "x_rows", "x_cols", "t_col", "b_t", "w1", "w1_t", "b1_c", "w2", "bias_rows", "l1_w", "l2_w",
        "l3_w", "ident", "rank_mats"]


def lay_out(x, adj, L0_gnn_t, L0_gnn_B, L0_gnn_W1, L0_gnn_b1, L0_gnn_W2, L0_gnn_b2, L1_gnn_weights,
            L1_gnn_bias, L2_gnn_W, L2_gnn_b, L3_gnn_weight, L3_gnn_bias):
    import numpy as np
    P, BLK = 128, 1024
    c = np.ascontiguousarray
    x, adj = np.asarray(x), np.asarray(adj)
    N, D = x.shape
    NB, Q = N // BLK, BLK // P
    w1 = np.asarray(L0_gnn_W1)
    HID = w1.shape[1]
    later = np.tril(np.ones((P, P), np.float32), -1) - 127 * np.eye(P, dtype=np.float32)
    return {
        "at": c(adj.reshape(NB, BLK, NB, 4, Q // 4, P).transpose(0, 2, 3, 5, 4, 1)).reshape(
            NB * NB * 4, P, (Q // 4) * BLK),
        "x_rows": c(x.reshape(N // P, P, D).transpose(1, 0, 2)),
        "x_cols": c(x.T),
        "t_col": c(np.broadcast_to(np.asarray(L0_gnn_t).reshape(1, 1), (P, HID // P))),
        "b_t": c(np.asarray(L0_gnn_B).T),
        "w1": c(w1[:D]),
        "w1_t": c(w1[D].reshape(HID // P, P).T),
        "b1_c": c(np.asarray(L0_gnn_b1).reshape(HID // P, P).T),
        "w2": c(np.asarray(L0_gnn_W2).reshape(HID // P, P, D).transpose(1, 0, 2)),
        "bias_rows": c(np.broadcast_to(np.stack([np.asarray(b) for b in (
            L0_gnn_b2, L1_gnn_bias, L2_gnn_b, L3_gnn_bias)])[None], (P, 4, D))),
        "l1_w": c(np.asarray(L1_gnn_weights).transpose(1, 0, 2)),
        "l2_w": c(np.asarray(L2_gnn_W).reshape(2, D, D).transpose(1, 0, 2)).reshape(D, 2 * D),
        "l3_w": c(np.asarray(L3_gnn_weight)),
        "ident": np.eye(P, dtype=np.float32),
        "rank_mats": c(np.stack([later, 1 - later], 1)),
    }


def build(nc, arrays, N, D):
    args = [nc.dram_tensor(f"in_{n}", arrays[n].shape, mybir.dt.float32, kind="ExternalInput").ap() for n in _INS]
    out = nc.dram_tensor("out_0", (N // 1024, 128, 8, D), mybir.dt.float32, kind="ExternalOutput").ap()
    graph_layers(nc, *args, out)


def kernel(**inputs):
    import numpy as np
    import concourse.bacc as bacc
    from concourse.bass_utils import run_bass_kernel_spmd

    arrays = lay_out(**inputs)
    N, D = inputs["x"].shape
    nc = bacc.Bacc("TRN2", target_bir_lowering=False, num_devices=1)
    build(nc, arrays, N, D)
    r = run_bass_kernel_spmd(nc, [{f"in_{n}": a for n, a in arrays.items()}], core_ids=[0])
    return np.ascontiguousarray(np.asarray(r.results[0]["out_0"]).transpose(0, 2, 1, 3)).reshape(N, D)
```

```python
import concourse.bass as bass
from concourse import mybir
from concourse.alu_op_type import AluOpType as ALU


def spend(eng, sem, n=1):
    eng.sem_inc(sem, -n)


def graph_layers(nc, at, x_rows, x_cols, t_col, b_t, w1, w1_t, b1_c, w2, bias_rows, l1_w, l2_w, l3_w,
                 ident, rank_mats, out):
    f32, f32r, bf16, u16 = mybir.dt.float32, mybir.dt.float32r, mybir.dt.bfloat16, mybir.dt.uint16
    ACT = mybir.ActivationFunctionType
    AX = mybir.AxisListType.X

    P = 128
    D = x_cols.shape[0]
    N = x_cols.shape[1]
    BLK = 1024
    NB = N // BLK
    G = N // P
    Q = BLK // P
    NQ = 4
    SUB = Q // NQ
    RING = 4
    HALF = 512
    HID = w1.shape[1]
    HC = HID // P
    EPS = 1e-5
    L2_EPS = 1e-12
    CUT = 100
    MARK = 127
    SCALE = float(2 ** (127 - CUT))

    at_off = [nc.sbuf_base]

    def place(name, shape, dt, at_byte=None):
        size = 4 if dt in (f32, f32r) else 2
        for n in shape[1:]:
            size *= n
        off = (at_off[0] + 31) // 32 * 32 if at_byte is None else at_byte
        if at_byte is None:
            at_off[0] = off + size
        return nc.alloc_sbuf_tensor_at(name, shape, dt, offset=off), off

    T, T_at = place("T", [P, 2, G, P], f32r)
    SV, SV_at = place("SV", [P, N], f32)
    O, _ = place("O", [P, G, D], f32)
    raw, raw_at = place("raw", [P, NQ, SUB, BLK], f32)
    hi, hi_at = place("hi", [P, RING, BLK], f32r)
    lo, lo_at = place("lo", [P, RING, BLK], f32r)
    st, _ = place("st", [P, 2, 2, SUB, P], f32r)
    UT, UT_at = place("UT", [P, BLK], f32)
    TT, _ = place("TT", [D, BLK], f32)
    xr, _ = place("xr", [P, Q, D], f32)
    hT, hT_at = place("hT", [P, HC, BLK], f32)
    xo, _ = place("xo", [P, Q, D], f32, hT_at + 4 * BLK)
    sq, _ = place("sq", [P, Q, D], f32, hT_at + 4 * BLK + 4 * Q * D)
    w1_sb, _ = place("w1_sb", [D, HID], f32)
    w2_sb, _ = place("w2_sb", [P, HC, D], f32)
    bt_sb, _ = place("bt_sb", [D, D], f32)
    hb_sb, _ = place("hb_sb", [P, 3, HC], f32)
    eye, _ = place("eye", [P, P], f32)
    pick1, _ = place("pick1", [P, D + 1], f32)
    comb, _ = place("comb", [P, 2 * D], f32)
    comb4, _ = place("comb4", [P, D], f32)
    w02, _ = place("w02", [D, D], f32)
    l2w_sb, _ = place("l2w_sb", [D, 2 * D], f32)
    l3w_sb, _ = place("l3w_sb", [D, D], f32)
    ones_st, _ = place("ones_st", [P, P], f32r)
    zst, _ = place("zst", [P, P], bf16)
    zmv, _ = place("zmv", [P, HALF], bf16)
    rank_b, _ = place("rank_b", [P, 2, P], bf16)
    bias, _ = place("bias", [P, 4, D], f32)
    RS, _ = place("RS", [P, G], f32)
    RD, _ = place("RD", [P, G], f32)
    st1, _ = place("st1", [P, Q], f32)
    st2, _ = place("st2", [P, Q], f32)
    st3, _ = place("st3", [P, Q], f32)
    relu_bias, _ = place("relu_bias", [P, 1], f32)
    spare, _ = place("spare", [P, 1], f32)
    l1w_sb, _ = place("l1w_sb", [P, 4, D], f32, UT_at)
    rank_f, _ = place("rank_f", [P, 2, P], f32, UT_at + 16 * D)
    S_ov, _ = place("S_ov", [P, 2, G, 2 * P], bf16, T_at)
    S, _ = place("S", [P, G, 3 * D], bf16, SV_at)
    M, _ = place("M", [P, 4, BLK], bf16, hi_at)
    Wt, _ = place("Wt", [P, 2, BLK], u16, lo_at)
    assert at_off[0] <= nc.sbuf_usable_end, at_off

    sem = nc.alloc_semaphore

    raw_ready = [sem(f"raw_ready{k}") for k in range(NQ)]
    raw_free = [sem(f"raw_free{k}") for k in range(NQ)]
    hi_ready = [sem(f"hi_ready{b}") for b in range(RING)]
    hi_free = [sem(f"hi_free{b}") for b in range(RING)]
    lo_done = sem("lo_done")
    lo_ready = [sem(f"lo_ready{b}") for b in range(RING)]
    lo_free = [sem(f"lo_free{b}") for b in range(RING)]
    st_ready = [sem(f"st_ready{k}") for k in range(2)]
    st_free = [sem(f"st_free{k}") for k in range(2)]
    b_done, b_free = sem("b_done"), sem("b_free")
    a_done, a_free = sem("a_done"), sem("a_free")
    evac_done = sem("evac_done")
    ut_ready = sem("ut_ready")
    fin_ready = sem("fin_ready")
    fin2_ready = sem("fin2_ready")
    xo_ready, xr_pe = sem("xo_ready"), sem("xr_pe")
    sums_ready = sem("sums_ready")
    v_ready = sem("v_ready")
    tp_ready = sem("tp_ready")
    tt_ready = sem("tt_ready")
    var_ready, sd_ready = sem("var_ready"), sem("sd_ready")
    dve_chain, pool_chain = sem("dve_chain"), sem("pool_chain")
    c_hid, c_x, c_rest = sem("c_hid"), sem("c_x"), sem("c_rest")
    c_hid2, c_rest2 = sem("c_hid2"), sem("c_rest2")
    h_ready, tanh_ready = sem("h_ready"), sem("tanh_ready")
    x_ready = sem("x_ready")
    hb_ready = sem("hb_ready")
    pool_const = sem("pool_const")
    t_start, const_ready = sem("t_start"), sem("const_ready")
    s_copied = sem("s_copied")
    m_ready = [sem(f"m_ready{k}") for k in range(2)]
    m_free = [sem(f"m_free{k}") for k in range(4)]
    r_ready = [sem(f"r_ready{k}") for k in range(2)]
    w_ready = [sem(f"w_ready{k}") for k in range(2)]
    w_free = [sem(f"w_free{k}") for k in range(2)]
    o_done, o_free = sem("o_done"), sem("o_free")
    out_ready, out_free, out_all = sem("out_ready"), sem("out_free"), sem("out_all")

    PSAB = nc.alloc_psum_tensor("PSAB", [P, 4, HALF], f32)
    PSA = PSAB[:, 0:2, :].rearrange("p h n -> p (h n)")
    PSB = PSAB[:, 2:4, :].rearrange("p h n -> p (h n)")
    PSF = nc.alloc_psum_tensor("PSF", [P, Q, P], f32)
    PST = nc.alloc_psum_tensor("PST", [P, BLK], f32)[:]
    PSF_flat = PSF[:].rearrange("p q n -> p (q n)")

    def ph(slot):
        return slice(D * slot, D * slot + D)

    def u_slot(k):
        return (k - 1) % 2

    def block_of(k, r):
        return r if k % 2 else NB - 1 - r

    def sweep_rows(eng, k, row):
        row(k, 0, None if k == 1 else (k - 1, block_of(k - 1, NB - 1)), k == 1, False, False)
        if k > 1 or NB > 2:
            row(k, 1, (k, block_of(k, 0)), k == 1, False, True)
        if NB > (3 if k == 1 else 2):
            with eng.Fori(2, NB - 1 if k == 1 else NB) as r:
                row(k, r, (k, block_of(k, r - 1)), k == 1, True, True)
        if k == 1:
            row(k, NB - 1, (k, block_of(k, NB - 2)), False, NB > 2, True)

    def above(eng, r, unit):
        with eng.Fori(r + 1, NB) as J:
            unit(J)

    def older_units(eng, k, r, unit):
        if k % 2:
            with eng.Fori(0, r - 1) as J:
                unit(J)
        else:
            with eng.Fori(0, r - 1) as o:
                unit(NB - 1 - o)

    with nc.Block() as block:

        @block.sync
        def _(sp):
            sp.dma_start(O[:], x_rows).then_inc(c_x, 16)
            sp.dma_start(bias[:], bias_rows).then_inc(c_x, 16)
            for k in range(NQ):
                sp.sem_inc(raw_free[k], 1)

            def load(I, J, quarters=range(NQ)):
                for k, q in enumerate(quarters):
                    sp.wait_ge(raw_free[k], 1)
                    spend(sp, raw_free[k])
                    sp.dma_start(raw[:, k], at[bass.ds((I * NB + J) * NQ + q, 1)].rearrange(
                        "o p (s i) -> (o p) s i", s=SUB)).then_inc(raw_ready[k], 16)

            def row(k, r, prev, upper, older, newest):
                I = block_of(k, r)
                load(I, I)
                if upper:
                    above(sp, r, lambda J: load(I, J))
                if older:
                    older_units(sp, k, r, lambda J: load(I, J))
                if newest:
                    load(I, block_of(k, r - 1))

            for k in range(1, 6):
                sweep_rows(sp, k, row)
            with sp.Fori(0, NB) as I:
                with sp.Fori(0, NB) as o:
                    load(I, NB - 1 - o, range(NQ - 1, -1, -1))

        @block.gpsimd
        def _(pool):
            for n, src in enumerate((w1_t, b1_c, t_col)):
                pool.dma_start(hb_sb[:, n, :], src).then_inc(c_hid, 16)
            for lo_p in (0, D):
                pool.dma_start(l1w_sb[lo_p:lo_p + D], l1_w).then_inc(c_rest, 16)
            pool.dma_start(rank_f[:], rank_mats).then_inc(c_rest, 16)
            pool.dma_start(eye[:], ident).then_inc(c_rest, 16)
            for dst, src in ((w1_sb, w1), (w2_sb, w2), (bt_sb, b_t), (l2w_sb, l2_w), (l3w_sb, l3_w)):
                pool.dma_start(dst[:], src).then_inc(c_hid2, 16)
            pool.dma_start(SV[0:D, :], x_cols).then_inc(c_hid2, 16)
            def link(ins):
                ins.then_inc(pool_chain, 1)
                pool.wait_ge(pool_chain, 1)
                spend(pool, pool_chain)

            nc.gpsimd.memset(T[:, 0, :, ph(1)].bitcast(f32), 1.0)
            nc.gpsimd.memset(T[:, 1, :, ph(1)].bitcast(f32), 0.0)
            nc.gpsimd.memset(ones_st[:, ph(0)].bitcast(f32), 0.0)
            nc.gpsimd.memset(ones_st[:, ph(1)].bitcast(f32), 1.0)
            nc.gpsimd.memset(zst[:], 0.0)
            nc.gpsimd.memset(zmv[:], 0.0)
            link(nc.gpsimd.memset(pick1[:], 0.0))
            link(nc.gpsimd.memset(pick1[D:D + 1, D:D + 1], 1.0))
            pool.sem_inc(pool_const, 1)

        @block.scalar
        def _(act):
            for b in range(RING):
                act.sem_inc(hi_free[b], 1)
            act.sem_inc(st_free[0], 1)

            def prepare(k, J, quarters=range(NQ)):
                for q in quarters:
                    operand(k, J, q)
                    split_hi((q + 1) % NQ)

            def split_hi(q):
                act.wait_ge(raw_ready[q], 16)
                spend(act, raw_ready[q], 16)
                for s in range(SUB):
                    b = (q * SUB + s) % RING
                    act.wait_ge(hi_free[b], 1)
                    spend(act, hi_free[b])
                    nc.scalar.copy(hi[:, b], raw[:, q, s]).then_inc(hi_ready[b], 1)

            def operand(k, J, q):
                b = q % 2
                act.wait_ge(st_free[b], 1)
                spend(act, st_free[b])
                g = bass.ds(J * Q + q * SUB, SUB)
                if k == 5:
                    src, dst = T[:, :, g, ph(0)], st[:, b, :, :, ph(0)]
                else:
                    src, dst = T[:, :, g, :], st[:, b]
                nc.scalar.copy(dst, src.bitcast(f32)).then_inc(st_ready[b], 1)

            def hidden(k, I, c):
                if k == 1:
                    act.wait_ge(h_ready, 1)
                    spend(act, h_ready)
                    nc.scalar.activation(hT[:, c, :], PST, ACT.Tanh, bias=hb_sb[:, 0, c:c + 1]).then_inc(
                        tanh_ready, 1)
                    if c == 0:
                        nc.scalar.copy(TT[:], SV[0:D, bass.ds(I * BLK, BLK)]).then_inc(x_ready, 1)

            def evacuate(k, I):
                u, v = ph(u_slot(k)), ph(1 - u_slot(k))
                cols = bass.ds(I * BLK, BLK)
                if k == 1:
                    act.wait_ge(b_done, 1)
                    spend(act, b_done)
                    nc.scalar.copy(UT[:], PSB).then_inc(b_free, 1)
                    nc.scalar.copy(SV[v, cols], PSA[v, :]).then_inc(evac_done, 1)
                else:
                    act.wait_ge(a_done, 1)
                    spend(act, a_done)
                    nc.scalar.copy(UT[u, :], PSA[u, :]).then_inc(evac_done, 1)
                    if k < 5:
                        nc.scalar.copy(SV[v, cols], PSA[v, :]).then_inc(a_free, 1)

            def transposed(k, stage):
                if (k, stage) in ((5, 0), (5, 2), (1, 2)):
                    act.wait_ge(tp_ready, 1)
                    spend(act, tp_ready)
                    nc.scalar.copy(TT[:], PST[0:D, :]).then_inc(tt_ready, 1)

            def root():
                act.wait_ge(var_ready, 1)
                spend(act, var_ready)
                nc.scalar.activation(st2[:], st1[:], ACT.Sqrt).then_inc(sd_ready, 1)

            def row(k, r, prev, upper, older, newest):
                I = block_of(k, r)
                same = prev and prev[0] == k
                if prev and not same:
                    split_hi(1)
                    evacuate(*prev)
                    transposed(prev[0], 0)
                    hidden(*prev, 0)
                    hidden(*prev, 1)
                    if prev[0] in (1, 4):
                        root()
                    transposed(prev[0], 2)
                    act.wait_ge(v_ready, 1)
                    spend(act, v_ready)
                    operand(k, I, 0)
                    operand(k, I, 1)
                else:
                    prepare(k, I, (0,))
                    if same:
                        evacuate(*prev)
                        transposed(k, 0)
                        hidden(*prev, 0)
                    operand(k, I, 1)
                    if same:
                        hidden(*prev, 1)
                        if k == 1:
                            nc.scalar.activation(spare[:], relu_bias[:], ACT.Sqrt, scale=0.0)
                split_hi(2)
                prepare(k, I, (2, 3))
                if upper:
                    above(act, r, lambda J: prepare(k, J))
                if older:
                    older_units(act, k, r, lambda J: prepare(k, J))
                if same:
                    if k in (1, 4, 5):
                        root()
                    if k < 5:
                        act.wait_ge(v_ready, 1)
                        spend(act, v_ready)
                if newest:
                    prepare(k, block_of(k, r - 1), (0, 1))
                    if k == 5:
                        root()
                    prepare(k, block_of(k, r - 1), (2, 3))
                if same:
                    transposed(k, 2)

            act.wait_ge(pool_const, 1)
            act.wait_ge(t_start, 1)
            split_hi(0)
            for k in range(1, 6):
                sweep_rows(act, k, row)
            evacuate(5, block_of(5, NB - 1))
            transposed(5, 0)
            root()
            root()
            transposed(5, 2)
            act.sem_inc(raw_ready[0], 16)

            for b in range(2):
                act.sem_inc(w_free[b], 1)

            def weights(first=range(Q)):
                for n in first:
                    b = n % 2
                    act.wait_ge(r_ready[b], 1)
                    spend(act, r_ready[b])
                    act.wait_ge(w_free[b], 1)
                    spend(act, w_free[b])
                    nc.scalar.activation(Wt[:, b, :], (PSF_flat, PST)[b], ACT.Relu, scale=-128.0,
                                         bias=relu_bias[:, 0:1]).then_inc(w_ready[b], 1)

            def store(I):
                act.wait_ge(out_ready, 1)
                spend(act, out_ready)
                act.dma_start(out[bass.ds(I, 1)].rearrange("o p q d -> (o p) q d"), xr[:]).then_inc(out_all, 16)
                act.wait_ge(out_all, 16)
                spend(act, out_all, 16)
                act.sem_inc(out_free, 1)

            weights()
            with act.Fori(1, NB):
                weights()
            with act.Fori(1, NB) as I:
                weights(range(0, 3))
                root()
                weights(range(3, Q))
                store(I - 1)
                with act.Fori(1, NB):
                    weights()
            root()
            store(NB - 1)

        @block.vector
        def _(dve):
            def link(ins):
                ins.then_inc(dve_chain, 1)
                dve.wait_ge(dve_chain, 1)
                spend(dve, dve_chain)

            def rows(col):
                return col.unsqueeze(2).broadcast_to([P, Q, D])

            def feats(row):
                return row.unsqueeze(1).broadcast_to([P, Q, D])

            for b in range(RING):
                dve.sem_inc(lo_free[b], 1)
            tt, ts = nc.vector.tensor_tensor, nc.vector.tensor_scalar
            stt, copy = nc.vector.scalar_tensor_tensor, nc.vector.tensor_copy

            dve.wait_ge(c_x, 32)
            link(copy(T[:, 0, :, ph(0)], O[:]))
            link(tt(T[:, 1, :, ph(0)], O[:], T[:, 0, :, ph(0)].bitcast(f32), ALU.subtract))
            dve.wait_ge(c_hid, 48)
            tt(O[:], O[:], bias[:, 0, :].unsqueeze(1).broadcast_to([P, G, D]), ALU.add)
            link(tt(hb_sb[:, 0, :], hb_sb[:, 0, :], hb_sb[:, 2, :], ALU.mult))
            tt(hb_sb[:, 0, :], hb_sb[:, 0, :], hb_sb[:, 1, :], ALU.add).then_inc(t_start, 1)
            dve.wait_ge(c_rest, 64)
            dve.wait_ge(c_hid2, 96)
            dve.wait_ge(pool_const, 1)
            a0, a1 = ph(0), ph(1)
            copy(rank_b[:], rank_f[:])
            copy(pick1[a0, 0:D], bt_sb[:])
            tt(w02[:], l1w_sb[a0, 0, :], l1w_sb[a0, 2, :], ALU.subtract)
            copy(comb[a1, 0:D], eye[a1, D:2 * D])
            tt(comb[a1, D:2 * D], l1w_sb[a1, 1, :], l1w_sb[a1, 3, :], ALU.subtract)
            ts(comb[a0, 0:D], eye[a0, 0:D], 2.0, None, ALU.mult)
            ts(comb[a0, D:2 * D], l1w_sb[a0, 2, :], 2.0, None, ALU.mult)
            nc.vector.memset(relu_bias[:], float(128 * (CUT - MARK)))
            ts(comb4[a1, :], l1w_sb[a1, 3, :], 2.0, None, ALU.mult).then_inc(const_ready, 1)

            def split_lo(quarters, sums=False):
                for q in quarters:
                    for s in range(SUB):
                        b = (q * SUB + s) % RING
                        dve.wait_ge(hi_ready[b], 1)
                        spend(dve, hi_ready[b])
                        dve.wait_ge(lo_free[b], 1)
                        spend(dve, lo_free[b])
                        ins = tt(lo[:, b], raw[:, q, s], hi[:, b].bitcast(f32), ALU.subtract)
                        if sums or s < SUB - 1:
                            ins.then_inc(lo_ready[b], 1)
                        else:
                            ins.then_inc(lo_done, 1)
                    if sums:
                        tt(UT[:], UT[:], raw[:, q, SUB - 1], ALU.add).then_inc(lo_done, 1)
                    dve.wait_ge(lo_done, 1)
                    spend(dve, lo_done)
                    if not sums:
                        dve.sem_inc(lo_ready[b], 1)
                    dve.sem_inc(raw_free[q], 1)

            def add_partial(k, I):
                u = ph(u_slot(k))
                dve.wait_ge(evac_done, 1)
                spend(dve, evac_done)
                if k == 1:
                    tt(UT[u, :], UT[u, :], PSA[u, :], ALU.add).then_inc(ut_ready, 1)
                else:
                    tt(UT[u, :], UT[u, :], SV[u, bass.ds(I * BLK, BLK)], ALU.add).then_inc(ut_ready, 1)

            def add_diagonal(k, I):
                if k > 1:
                    u, cols = ph(u_slot(k)), bass.ds(I * BLK, BLK)
                    dve.wait_ge(b_done, 1)
                    spend(dve, b_done)
                    link(tt(SV[u, cols], SV[u, cols], PSB[u, :], ALU.add))
                    dve.sem_inc(b_free, 1)

            def centre():
                link(nc.vector.tensor_reduce(st1[:], xr[:], AX, ALU.add))
                link(stt(xr[:], rows(st1[:]), -1.0 / D, xr[:], ALU.mult, ALU.add))
                link(tt(sq[:], xr[:], xr[:], ALU.mult))
                link(nc.vector.tensor_reduce(st1[:], sq[:], AX, ALU.add))
                ts(st1[:], st1[:], 1.0 / D, EPS, ALU.mult, ALU.add).then_inc(var_ready, 1)

            def scale():
                dve.wait_ge(sd_ready, 1)
                spend(dve, sd_ready)
                link(nc.vector.reciprocal(st3[:], st2[:]))
                return tt(xr[:], xr[:], rows(st3[:]), ALU.mult)

            def whole(k, I):
                if k in (3, 5):
                    src = T[:, :, bass.ds(I * Q, Q), ph(1 if k == 3 else 0)].bitcast(f32)
                    ins = tt(xo[:], src[:, 0], src[:, 1], ALU.add)
                    if k == 5:
                        ins.then_inc(xo_ready, 1)
                    else:
                        link(ins)

            def write_v(k, I):
                dst = T[:, :, bass.ds(I * Q, Q), ph(1 - u_slot(k))]
                link(copy(dst[:, 0], xr[:]))
                tt(dst[:, 1], xr[:], dst[:, 0].bitcast(f32), ALU.subtract).then_inc(v_ready, 1)

            def finish_first(k, I):
                g = bass.ds(I * Q, Q)
                f0, f1 = PSF[:, :, 0:D], PSF[:, :, D:2 * D]
                dve.wait_ge(fin_ready, 1)
                spend(dve, fin_ready)
                if k == 1:
                    link(copy(RS[:, g], PSF[:, :, D]))
                    link(tt(sq[:], PST[:, 0:Q * D].rearrange("p (q d) -> p q d", q=Q), rows(RS[:, g]), ALU.mult))
                    link(tt(xr[:], f0, sq[:], ALU.subtract))
                    tt(xr[:], xr[:], O[:, g, :], ALU.add).then_inc(dve_chain, 1)
                    dve.wait_ge(dve_chain, 1)
                    spend(dve, dve_chain)
                elif k == 2:
                    link(copy(xr[:], f0))
                elif k == 3:
                    link(tt(xr[:], f0, xo[:], ALU.subtract))
                elif k == 4:
                    link(tt(xr[:], f0, O[:, g, :], ALU.add))
                    centre()
                else:
                    link(tt(sq[:], f1, rows(RD[:, g]), ALU.mult))
                    link(tt(xr[:], f0, sq[:], ALU.add))
                    link(tt(xr[:], xr[:], feats(bias[:, 2, :]), ALU.add))
                    link(stt(sq[:], xr[:], 0.0, xr[:], ALU.max, ALU.mult))
                    nc.vector.tensor_reduce(st1[:], sq[:], AX, ALU.add).then_inc(var_ready, 1)

            def finish_middle(k):
                if k == 1:
                    centre()

            def finish_last(k, I):
                if k == 1:
                    link(scale())
                    dve.sem_inc(xr_pe, 1)
                    write_v(k, I)
                elif k in (2, 3):
                    write_v(k, I)
                elif k == 4:
                    link(scale())
                    write_v(k, I)
                elif k == 5:
                    dve.wait_ge(sd_ready, 1)
                    spend(dve, sd_ready)
                    link(ts(st3[:], st2[:], L2_EPS, None, ALU.max))
                    link(nc.vector.reciprocal(st3[:], st3[:]))
                    link(stt(xr[:], xr[:], 0.0, rows(st3[:]), ALU.max, ALU.mult))
                    link(tt(xr[:], xr[:], xo[:], ALU.add))

            def outputs(k, I):
                if k in (2, 3):
                    g = bass.ds(I * Q, Q)
                    link(tt(O[:, g, :], O[:, g, :], PSF[:, :, D:2 * D], ALU.add))

            def norm_first(k):
                if k == 5:
                    centre()

            def norm_last(k, I):
                if k == 5:
                    link(scale())
                    copy(O[:, bass.ds(I * Q, Q), :], xr[:]).then_inc(xr_pe, 1)

            def after(k, I):
                g = bass.ds(I * Q, Q)
                if k == 1:
                    link(ts(RD[:, g], RS[:, g], 1.0, 1.0, ALU.add, ALU.max))
                    nc.vector.reciprocal(RD[:, g], RD[:, g])
                    dve.wait_ge(fin2_ready, 1)
                    spend(dve, fin2_ready)
                    link(tt(O[:, g, :], xr[:], PSF[:, :, 0:D], ALU.add))
                    link(tt(O[:, g, :], O[:, g, :], feats(bias[:, 1, :]), ALU.add))
                elif k == 5:
                    s1, s2, s3 = S_ov[:, 0, g, P:P + D], S_ov[:, 0, g, P + D:2 * P], S_ov[:, 1, g, P:P + D]
                    dve.wait_ge(fin2_ready, 1)
                    spend(dve, fin2_ready)
                    link(ts(sq[:], PSF[:, :, 0:D], SCALE, None, ALU.mult))
                    link(copy(s1, sq[:]))
                    link(tt(sq[:], sq[:], s1, ALU.subtract))
                    link(copy(s2, sq[:]))
                    link(tt(s3, sq[:], s2, ALU.subtract))

            def row(k, r, prev, upper, older, newest):
                same = prev and prev[0] == k
                if prev:
                    whole(*prev)
                split_lo((0, 1))
                if prev:
                    add_partial(*prev)
                if prev and not same:
                    finish_first(*prev)
                    finish_middle(prev[0])
                    finish_last(*prev)
                    outputs(*prev)
                    after(*prev)
                split_lo((2, 3))
                if same:
                    finish_first(*prev)
                if upper:
                    above(dve, r, lambda J: split_lo(range(NQ)))
                sums = k == 1
                if newest and sums:
                    link(nc.vector.memset(UT[:], 0.0))
                if same:
                    finish_middle(k)
                if older:
                    older_units(dve, k, r, lambda J: split_lo(range(NQ), sums))
                if same:
                    finish_last(*prev)
                if newest:
                    split_lo((0,), sums)
                    outputs(*prev)
                    norm_first(k)
                    split_lo((1,), sums)
                    norm_last(*prev)
                    split_lo((2,), sums)
                    add_diagonal(k, block_of(k, r))
                    split_lo((3,), sums)
                if newest and sums:
                    dve.sem_inc(sums_ready, 1)
                if same:
                    after(*prev)
                if not newest:
                    add_diagonal(k, block_of(k, r))

            for k in range(1, 6):
                sweep_rows(dve, k, row)
            last = block_of(5, NB - 1)
            whole(5, last)
            add_partial(5, last)
            finish_first(5, last)
            finish_last(5, last)
            norm_first(5)
            norm_last(5, last)
            after(5, last)

            copy(S[:, :, 0:2 * D], S_ov[:, 0, :, P:2 * P])
            copy(S[:, :, 2 * D:3 * D], S_ov[:, 1, :, P:P + D]).then_inc(s_copied, 1)
            for b in range(SUB):
                dve.wait_ge(hi_ready[b], 1)
                spend(dve, hi_ready[b])
            dve.sem_inc(m_free[1], 1)
            dve.sem_inc(m_free[2], 1)
            dve.sem_inc(out_free, 1)

            def count(k, first=False):
                dve.wait_ge(raw_ready[k], 16)
                spend(dve, raw_ready[k], 16)
                for n in (k * SUB, k * SUB + 1):
                    old, new = n % 4, (n + 1) % 4
                    dve.wait_ge(m_free[new], 1)
                    spend(dve, m_free[new])
                    src = raw[:, k, SUB - 1 - n % 2, :]
                    if first and n == 0:
                        ins = ts(M[:, new, :], src, 0.0, None, ALU.not_equal)
                    else:
                        ins = stt(M[:, new, :], src, 0.0, M[:, old, :], ALU.not_equal, ALU.add)
                    ins.then_inc(lo_done, 1)
                    dve.wait_ge(lo_done, 1)
                    spend(dve, lo_done)
                    dve.sem_inc(m_ready[n % 2], 1)
                dve.sem_inc(raw_free[k], 1)

            def gather(I):
                dve.wait_ge(o_done, 1)
                spend(dve, o_done)
                dve.wait_ge(out_free, 1)
                spend(dve, out_free)
                link(nc.vector.tensor_reduce(
                    xr[:].rearrange("p (a b) d -> p a b d", b=2),
                    PSAB[:, :, 0:6 * D].rearrange("p a (b t d) -> p a b d t", b=2, t=3), AX, ALU.add))
                dve.sem_inc(o_free, 1)
                link(tt(xr[:], xr[:], feats(bias[:, 3, :]), ALU.add))
                link(tt(xr[:], xr[:], O[:, bass.ds(I * Q, Q), :], ALU.add))

            def counts(I, prev):
                count(0, first=True)
                if prev is not None:
                    gather(prev)
                count(1)
                if prev is not None:
                    centre()
                count(2)
                if prev is not None:
                    scale().then_inc(out_ready, 1)
                count(3)
                with dve.Fori(1, NB):
                    for k in range(NQ):
                        count(k)

            counts(0, None)
            with dve.Fori(1, NB) as I:
                counts(I, I - 1)
            gather(NB - 1)
            centre()
            scale().then_inc(out_ready, 1)

        @block.tensor
        def _(pe):
            mm = nc.tensor.matmul

            def small(dst, lhs, rhs, **kw):
                for q in range(Q):
                    last = mm(dst[:, q, :], lhs[:, q * P:(q + 1) * P], rhs, start=True, stop=True)
                return last

            pe.sem_inc(b_free, 1)
            pe.sem_inc(a_free, 1)
            pe.wait_ge(pool_const, 1)
            pe.wait_ge(const_ready, 1)

            def multiply(bank, quarters=range(NQ), sums_bank=None, start=False, stop=False):
                for q in quarters:
                    pe.wait_ge(st_ready[q % 2], 1)
                    spend(pe, st_ready[q % 2])
                    for s in range(SUB):
                        b = (q * SUB + s) % RING
                        first, last = start and q + s == 0, stop and q == NQ - 1 and s == SUB - 1
                        w_hi, w_lo = st[:, q % 2, 0, s, :], st[:, q % 2, 1, s, :]
                        pe.wait_ge(lo_ready[b], 1)
                        spend(pe, lo_ready[b])
                        rows_too = sums_bank is not None and s < SUB - 1
                        terms = [(bank, w_hi, lo)] + [(sums_bank, ones_st[:], lo)] * rows_too
                        n_lo = 2 * len(terms)
                        terms += [(bank, w_hi, hi), (bank, w_lo, hi)]
                        terms += [(sums_bank, ones_st[:], hi)] * rows_too
                        for n in range(2 * len(terms)):
                            dst, w, src = terms[n // 2]
                            cols = slice(n % 2 * HALF, (n % 2 + 1) * HALF)
                            ins = mm(dst[:, cols], w, src[:, b, cols], start=first and n < 2,
                                     stop=last and n >= 2 * len(terms) - 2)
                            if n == 0 and s == 0:
                                ins.then_inc(st_free[(q - 1) % 2], 1)
                            elif n == n_lo - 1:
                                ins.then_inc(lo_free[b], 1)
                            elif n == 2 * len(terms) - 1:
                                ins.then_inc(hi_free[b], 1)

            def zeros(bank, start):
                for h in range(2):
                    last = mm(bank[:, h * HALF:(h + 1) * HALF], zst[:], zmv[:], start=start, stop=not start)
                return last

            def transpose(src):
                for q in range(Q):
                    last = mm(PST[0:D, q * P:(q + 1) * P], src[:, q, :], eye[:], start=True, stop=True)
                last.then_inc(tp_ready, 1)

            def hidden(k, I, c):
                if k == 1:
                    if c > 0:
                        pe.wait_ge(tanh_ready, 1)
                        spend(pe, tanh_ready)
                    for h in range(2):
                        last = mm(PST[:, h * HALF:(h + 1) * HALF], w1_sb[:, c * P:(c + 1) * P],
                                  SV[0:D, bass.ds(I * BLK + h * HALF, HALF)], start=True, stop=True)
                    last.then_inc(h_ready, 1)

            def end0(k, I):
                if k == 5:
                    pe.wait_ge(xo_ready, 1)
                    spend(pe, xo_ready)
                    transpose(xo)

            def end1(k, I):
                u = ph(u_slot(k))
                pe.wait_ge(ut_ready, 1)
                spend(pe, ut_ready)
                if k == 1:
                    pe.wait_ge(tanh_ready, 1)
                    spend(pe, tanh_ready)
                    pe.wait_ge(x_ready, 1)
                    spend(pe, x_ready)
                    for q in range(Q):
                        cols = slice(q * P, (q + 1) * P)
                        mm(PSF[:, q, 0:D + 1], UT[:, cols], pick1[:], start=True, stop=False)
                        for c in range(HC):
                            mm(PSF[:, q, 0:D], hT[:, c, cols], w2_sb[:, c, :], start=False, stop=c == HC - 1)
                        last = mm(PST[:, q * D:(q + 1) * D], TT[:, cols], bt_sb[:], start=True, stop=True)
                elif k < 4:
                    last = small(PSF, UT[u, :], comb[u, :])
                elif k == 4:
                    last = small(PSF[:, :, 0:D], UT[u, :], comb4[u, :])
                else:
                    pe.wait_ge(tt_ready, 1)
                    spend(pe, tt_ready)
                    for q in range(Q):
                        mm(PSF[:, q, :], TT[:, q * P:(q + 1) * P], l2w_sb[:], start=True, stop=False)
                        last = mm(PSF[:, q, D:2 * D], UT[u, q * P:(q + 1) * P], l2w_sb[:, D:2 * D],
                                  start=False, stop=True)
                last.then_inc(fin_ready, 1)

            def end2(k, I):
                if k in (1, 5):
                    pe.wait_ge(xr_pe, 1)
                    spend(pe, xr_pe)
                    transpose(xr)

            def end3(k, I):
                if k in (1, 5):
                    pe.wait_ge(tt_ready, 1)
                    spend(pe, tt_ready)
                    small(PSF[:, :, 0:D], TT, w02[:] if k == 1 else l3w_sb[:]).then_inc(fin2_ready, 1)

            def row(k, r, prev, upper, older, newest):
                same = prev and prev[0] == k
                sums = PSB if k == 1 else None
                if prev:
                    end0(*prev)
                    hidden(*prev, 0)
                if prev and not same:
                    hidden(*prev, 1)
                    end1(*prev)
                    end2(*prev)
                    end3(*prev)
                pe.wait_ge(b_free, 1)
                spend(pe, b_free)
                multiply(PSB, (0,), start=True)
                if same:
                    hidden(*prev, 1)
                multiply(PSB, (1,))
                if same:
                    end1(*prev)
                multiply(PSB, (2, 3), stop=k > 1)
                if k > 1:
                    mm(PST[:, 0:2], zst[:], zmv[:, 0:2], start=True, stop=True).then_inc(b_done, 1)
                if upper:
                    above(pe, r, lambda J: multiply(PSB))
                if 2 <= k <= 4 or (k == 5 and not same):
                    pe.wait_ge(a_free, 1)
                    spend(pe, a_free)
                zeros(PSA, True)
                if older:
                    older_units(pe, k, r, lambda J: multiply(PSA, sums_bank=sums))
                if newest:
                    multiply(PSA, (0, 1), sums_bank=sums)
                    if k == 1:
                        end2(*prev)
                    multiply(PSA, (2, 3), sums_bank=sums)
                if same:
                    if k == 5:
                        end2(*prev)
                    end3(*prev)
                last = zeros(PSA, False)
                if k == 1:
                    if newest:
                        pe.wait_ge(sums_ready, 1)
                        spend(pe, sums_ready)
                        for h in range(2):
                            last = mm(PSB[:, h * HALF:(h + 1) * HALF], ones_st[:].bitcast(f32),
                                      UT[:, h * HALF:(h + 1) * HALF], start=False, stop=True)
                    else:
                        last = zeros(PSB, False)
                    last.then_inc(b_done, 1)
                else:
                    last.then_inc(a_done, 1)

            for k in range(1, 6):
                sweep_rows(pe, k, row)
            last = block_of(5, NB - 1)
            end0(5, last)
            end1(5, last)
            end2(5, last)
            end3(5, last)

            pe.wait_ge(s_copied, 1)
            spend(pe, s_copied)
            pe.sem_inc(o_free, 1)
            ranks = (PSF_flat, PST)

            def rank(n, first=False):
                b, old, new = n % 2, n % 4, (n + 1) % 4
                pe.wait_ge(m_ready[b], 1)
                spend(pe, m_ready[b])
                terms = [(0, new, h) for h in range(2)] + [(1, old, h) for h in range(2)] * (not first)
                for i, (m, src, h) in enumerate(terms):
                    ins = mm(ranks[b][:, h * HALF:(h + 1) * HALF], rank_b[:, m, :],
                             M[:, src, h * HALF:(h + 1) * HALF], start=i < 2, stop=i >= len(terms) - 2)
                    if i == 0:
                        ins.then_inc(m_free[(n - 1) % 4], 1)
                    elif i == len(terms) - 1:
                        ins.then_inc(r_ready[b], 1)

            def weigh(n, J):
                b = n % 2
                pe.wait_ge(w_ready[b], 1)
                spend(pe, w_ready[b])
                g = J * Q + (Q - 1 - n)
                for q in range(Q):
                    last = mm(PSAB[:, q // 2, (q % 2) * 3 * D:(q % 2 + 1) * 3 * D],
                              Wt[:, b, q * P:(q + 1) * P].bitcast(bf16), S[:, bass.ds(g, 1), :].rearrange(
                                  "p o n -> p (o n)"), start=False, stop=False)
                last.then_inc(w_free[b], 1)

            def bounds(start):
                for a in range(4):
                    last = mm(PSAB[:, a, 0:6 * D], zst[:], zmv[:, 0:6 * D], start=start, stop=not start)
                return last

            with pe.Fori(0, NB) as I:
                rank(0, first=True)
                rank(1)
                pe.wait_ge(o_free, 1)
                spend(pe, o_free)
                bounds(True)
                weigh(0, NB - 1)
                for n in range(2, Q):
                    rank(n)
                    weigh(n - 1, NB - 1)
                with pe.Fori(1, NB) as o:
                    rank(0)
                    weigh(Q - 1, NB - o)
                    for n in range(1, Q):
                        rank(n)
                        weigh(n - 1, NB - 1 - o)
                weigh(Q - 1, 0)
                bounds(False).then_inc(o_done, 1)


_INS = ["at", "x_rows", "x_cols", "t_col", "b_t", "w1", "w1_t", "b1_c", "w2", "bias_rows", "l1_w", "l2_w",
        "l3_w", "ident", "rank_mats"]


def lay_out(x, adj, L0_gnn_t, L0_gnn_B, L0_gnn_W1, L0_gnn_b1, L0_gnn_W2, L0_gnn_b2, L1_gnn_weights,
            L1_gnn_bias, L2_gnn_W, L2_gnn_b, L3_gnn_weight, L3_gnn_bias):
    import numpy as np
    P, BLK = 128, 1024
    c = np.ascontiguousarray
    x, adj = np.asarray(x), np.asarray(adj)
    N, D = x.shape
    NB, Q = N // BLK, BLK // P
    w1 = np.asarray(L0_gnn_W1)
    HID = w1.shape[1]
    later = np.tril(np.ones((P, P), np.float32), -1) - 127 * np.eye(P, dtype=np.float32)
    return {
        "at": c(adj.reshape(NB, BLK, NB, 4, Q // 4, P).transpose(0, 2, 3, 5, 4, 1)).reshape(
            NB * NB * 4, P, (Q // 4) * BLK),
        "x_rows": c(x.reshape(N // P, P, D).transpose(1, 0, 2)),
        "x_cols": c(x.T),
        "t_col": c(np.broadcast_to(np.asarray(L0_gnn_t).reshape(1, 1), (P, HID // P))),
        "b_t": c(np.asarray(L0_gnn_B).T),
        "w1": c(w1[:D]),
        "w1_t": c(w1[D].reshape(HID // P, P).T),
        "b1_c": c(np.asarray(L0_gnn_b1).reshape(HID // P, P).T),
        "w2": c(np.asarray(L0_gnn_W2).reshape(HID // P, P, D).transpose(1, 0, 2)),
        "bias_rows": c(np.broadcast_to(np.stack([np.asarray(b) for b in (
            L0_gnn_b2, L1_gnn_bias, L2_gnn_b, L3_gnn_bias)])[None], (P, 4, D))),
        "l1_w": c(np.asarray(L1_gnn_weights).transpose(1, 0, 2)),
        "l2_w": c(np.asarray(L2_gnn_W).reshape(2, D, D).transpose(1, 0, 2)).reshape(D, 2 * D),
        "l3_w": c(np.asarray(L3_gnn_weight)),
        "ident": np.eye(P, dtype=np.float32),
        "rank_mats": c(np.stack([later, 1 - later], 1)),
    }


def build(nc, arrays, N, D):
    args = [nc.dram_tensor(f"in_{n}", arrays[n].shape, mybir.dt.float32, kind="ExternalInput").ap() for n in _INS]
    out = nc.dram_tensor("out_0", (N // 1024, 128, 8, D), mybir.dt.float32, kind="ExternalOutput").ap()
    graph_layers(nc, *args, out)


def kernel(**inputs):
    import numpy as np
    import concourse.bacc as bacc
    from concourse.bass_utils import run_bass_kernel_spmd

    arrays = lay_out(**inputs)
    N, D = inputs["x"].shape
    nc = bacc.Bacc("TRN2", target_bir_lowering=False, num_devices=1)
    build(nc, arrays, N, D)
    r = run_bass_kernel_spmd(nc, [{f"in_{n}": a for n, a in arrays.items()}], core_ids=[0])
    return np.ascontiguousarray(np.asarray(r.results[0]["out_0"]).transpose(0, 2, 1, 3)).reshape(N, D)
```

```python
import concourse.bass as bass
from concourse import mybir
from concourse.alu_op_type import AluOpType as ALU


def spend(eng, sem, n=1):
    eng.sem_inc(sem, -n)


def graph_layers(nc, at, x_rows, x_cols, t_col, b_t, w1, w1_t, b1_c, w2, bias_rows, l1_w, l2_w, l3_w,
                 ident, rank_mats, out):
    f32, f32r, bf16, u16 = mybir.dt.float32, mybir.dt.float32r, mybir.dt.bfloat16, mybir.dt.uint16
    ACT = mybir.ActivationFunctionType
    AX = mybir.AxisListType.X

    P = 128
    D = x_cols.shape[0]
    N = x_cols.shape[1]
    BLK = 1024
    NB = N // BLK
    G = N // P
    Q = BLK // P
    NQ = 4
    SUB = Q // NQ
    RING = 4
    HALF = 512
    HID = w1.shape[1]
    HC = HID // P
    EPS = 1e-5
    L2_EPS = 1e-12
    CUT = 100
    MARK = 127
    SCALE = float(2 ** (127 - CUT))

    at_off = [nc.sbuf_base]

    def place(name, shape, dt, at_byte=None):
        size = 4 if dt in (f32, f32r) else 2
        for n in shape[1:]:
            size *= n
        off = (at_off[0] + 31) // 32 * 32 if at_byte is None else at_byte
        if at_byte is None:
            at_off[0] = off + size
        return nc.alloc_sbuf_tensor_at(name, shape, dt, offset=off), off

    T, _ = place("T", [P, 2, G, P], f32r)
    SV, SV_at = place("SV", [P, N], f32)
    O, _ = place("O", [P, G, D], f32)
    raw, raw_at = place("raw", [P, NQ, SUB, BLK], f32)
    hi, hi_at = place("hi", [P, RING, BLK], f32r)
    lo, lo_at = place("lo", [P, RING, BLK], f32r)
    st, _ = place("st", [P, 2, 2, SUB, P], f32r)
    UT, UT_at = place("UT", [P, BLK], f32)
    TT, _ = place("TT", [D, BLK], f32)
    xr, _ = place("xr", [P, Q, D], f32)
    hT, hT_at = place("hT", [P, HC, BLK], f32)
    xo, _ = place("xo", [P, Q, D], f32, hT_at + 4 * BLK)
    sq, _ = place("sq", [P, Q, D], f32, hT_at + 4 * BLK + 4 * Q * D)
    w1_sb, _ = place("w1_sb", [D, HID], f32)
    w2_sb, _ = place("w2_sb", [P, HC, D], f32)
    bt_sb, _ = place("bt_sb", [D, D], f32)
    hb_sb, _ = place("hb_sb", [P, 3, HC], f32)
    eye, _ = place("eye", [P, P], f32)
    pick1, _ = place("pick1", [P, D + 1], f32)
    comb, _ = place("comb", [P, 2 * D], f32)
    comb4, _ = place("comb4", [P, D], f32)
    w02, _ = place("w02", [D, D], f32)
    l2w_sb, _ = place("l2w_sb", [D, 2 * D], f32)
    l3w_sb, _ = place("l3w_sb", [D, D], f32)
    ones_st, _ = place("ones_st", [P, P], f32r)
    zst, _ = place("zst", [P, P], bf16)
    zmv, _ = place("zmv", [P, HALF], bf16)
    rank_b, _ = place("rank_b", [P, 2, P], bf16)
    bias, _ = place("bias", [P, 4, D], f32)
    RS, _ = place("RS", [P, G], f32)
    RD, _ = place("RD", [P, G], f32)
    st1, _ = place("st1", [P, Q], f32)
    st2, _ = place("st2", [P, Q], f32)
    st3, _ = place("st3", [P, Q], f32)
    relu_bias, _ = place("relu_bias", [P, 1], f32)
    spare, _ = place("spare", [P, 1], f32)
    l1w_sb, _ = place("l1w_sb", [P, 4, D], f32, UT_at)
    rank_f, _ = place("rank_f", [P, 2, P], f32, UT_at + 16 * D)
    S, _ = place("S", [P, G, 3 * D], bf16, SV_at)
    M, _ = place("M", [P, Q, BLK], bf16, hi_at)
    Wt, _ = place("Wt", [P, 2, BLK], u16, lo_at)
    assert at_off[0] <= nc.sbuf_usable_end, at_off

    sem = nc.alloc_semaphore

    raw_ready = [sem(f"raw_ready{k}") for k in range(NQ)]
    raw_free = [sem(f"raw_free{k}") for k in range(NQ)]
    hi_ready = [sem(f"hi_ready{b}") for b in range(RING)]
    hi_free = [sem(f"hi_free{b}") for b in range(RING)]
    lo_done, sums_done = sem("lo_done"), sem("sums_done")
    lo_ready = [sem(f"lo_ready{b}") for b in range(RING)]
    lo_free = [sem(f"lo_free{b}") for b in range(RING)]
    st_ready = [sem(f"st_ready{k}") for k in range(2)]
    st_free = [sem(f"st_free{k}") for k in range(2)]
    b_done, b_free = sem("b_done"), sem("b_free")
    a_done, a_free = sem("a_done"), sem("a_free")
    evac_done = sem("evac_done")
    ut_ready = sem("ut_ready")
    fin_ready = sem("fin_ready")
    fin2_ready = sem("fin2_ready")
    ut_used = sem("ut_used")
    psf_free = sem("psf_free")
    xo_ready, xr_pe = sem("xo_ready"), sem("xr_pe")
    sums_ready = sem("sums_ready")
    v_ready = sem("v_ready")
    tp_ready = sem("tp_ready")
    tt_ready = sem("tt_ready")
    var_ready, sd_ready = sem("var_ready"), sem("sd_ready")
    dve_chain, pool_chain = sem("dve_chain"), sem("pool_chain")
    c_hid, c_x, c_rest = sem("c_hid"), sem("c_x"), sem("c_rest")
    c_hid2, c_rest2 = sem("c_hid2"), sem("c_rest2")
    h_ready, tanh_ready = sem("h_ready"), sem("tanh_ready")
    x_ready = sem("x_ready")
    hb_ready = sem("hb_ready")
    pool_const = sem("pool_const")
    t_start, const_ready = sem("t_start"), sem("const_ready")
    s_ready = sem("s_ready")
    half_done = [sem(f"half_done{h}") for h in range(2)]
    m_ready = [sem(f"m_ready{n}") for n in range(Q)]
    m_free = [sem(f"m_free{n}") for n in range(Q)]
    r_ready = [sem(f"r_ready{k}") for k in range(2)]
    w_ready = [sem(f"w_ready{k}") for k in range(2)]
    w_free = [sem(f"w_free{k}") for k in range(2)]
    o_done, o_free = sem("o_done"), sem("o_free")
    out_ready, out_all = sem("out_ready"), sem("out_all")

    PSAB = nc.alloc_psum_tensor("PSAB", [P, 4, HALF], f32)
    PSA = PSAB[:, 0:2, :].rearrange("p h n -> p (h n)")
    PSB = PSAB[:, 2:4, :].rearrange("p h n -> p (h n)")
    PSF = nc.alloc_psum_tensor("PSF", [P, Q, P], f32)
    PST = nc.alloc_psum_tensor("PST", [P, BLK], f32)[:]
    PSF_flat = PSF[:].rearrange("p q n -> p (q n)")

    def ph(slot):
        return slice(D * slot, D * slot + D)

    def u_slot(k):
        return (k - 1) % 2

    def block_of(k, r):
        return r if k % 2 else NB - 1 - r

    def sweep_rows(eng, k, row, peeled=2):
        row(k, 0, None if k == 1 else (k - 1, block_of(k - 1, NB - 1)), k == 1, False, False)
        if k > 1 or NB > 2:
            row(k, 1, (k, block_of(k, 0)), k == 1, False, True)
        if peeled > 2:
            row(k, 2, (k, block_of(k, 1)), k == 1, True, True)
        if NB - (k == 1) > peeled:
            with eng.Fori(peeled, NB - 1 if k == 1 else NB) as r:
                row(k, r, (k, block_of(k, r - 1)), k == 1, True, True)
        if k == 1:
            row(k, NB - 1, (k, block_of(k, NB - 2)), False, NB > 2, True)

    def above(eng, r, unit):
        with eng.Fori(r + 1, NB) as J:
            unit(J)

    def older_units(eng, k, r, unit):
        if k % 2:
            with eng.Fori(0, r - 1) as J:
                unit(J)
        else:
            with eng.Fori(0, r - 1) as o:
                unit(NB - 1 - o)

    with nc.Block() as block:

        @block.sync
        def _(sp):
            sp.dma_start(O[:], x_rows).then_inc(c_x, 16)
            sp.dma_start(bias[:], bias_rows).then_inc(c_x, 16)
            for k in range(NQ - 1):
                sp.sem_inc(raw_free[k], 1)

            def load(I, J, quarters=range(NQ)):
                for k, q in enumerate(quarters):
                    sp.wait_ge(raw_free[k], 1)
                    spend(sp, raw_free[k])
                    sp.dma_start(raw[:, k], at[bass.ds((I * NB + J) * NQ + q, 1)].rearrange(
                        "o p (s i) -> (o p) s i", s=SUB)).then_inc(raw_ready[k], 16)

            def row(k, r, prev, upper, older, newest):
                I = block_of(k, r)
                load(I, I)
                if upper:
                    above(sp, r, lambda J: load(I, J))
                if older:
                    older_units(sp, k, r, lambda J: load(I, J))
                if newest:
                    load(I, block_of(k, r - 1))

            for k in range(1, 6):
                sweep_rows(sp, k, row)
            with sp.Fori(0, NB) as I:
                with sp.Fori(0, NB) as o:
                    load(I, NB - 1 - o, range(NQ - 1, -1, -1))

        @block.gpsimd
        def _(pool):
            for n, src in enumerate((w1_t, b1_c, t_col)):
                pool.dma_start(hb_sb[:, n, :], src).then_inc(c_hid, 16)
            for lo_p in (0, D):
                pool.dma_start(l1w_sb[lo_p:lo_p + D], l1_w).then_inc(c_rest, 16)
            pool.dma_start(rank_f[:], rank_mats).then_inc(c_rest, 16)
            pool.dma_start(eye[:], ident).then_inc(c_rest, 16)
            for dst, src in ((w1_sb[:], w1), (w2_sb[:], w2), (bt_sb[:], b_t), (l2w_sb[:], l2_w),
                             (l3w_sb[:], l3_w)):
                pool.dma_start(dst, src).then_inc(c_hid2, 16)
            pool.dma_start(SV[0:D, :], x_cols).then_inc(c_hid2, 16)
            def link(ins):
                ins.then_inc(pool_chain, 1)
                pool.wait_ge(pool_chain, 1)
                spend(pool, pool_chain)

            nc.gpsimd.memset(T[:, 0, :, ph(1)].bitcast(f32), 1.0)
            nc.gpsimd.memset(T[:, 1, :, ph(1)].bitcast(f32), 0.0)
            nc.gpsimd.memset(ones_st[:, ph(0)].bitcast(f32), 0.0)
            nc.gpsimd.memset(ones_st[:, ph(1)].bitcast(f32), 1.0)
            nc.gpsimd.memset(zst[:], 0.0)
            nc.gpsimd.memset(zmv[:], 0.0)
            link(nc.gpsimd.memset(pick1[:], 0.0))
            link(nc.gpsimd.memset(pick1[D:D + 1, D:D + 1], 1.0))
            pool.sem_inc(pool_const, 1)

            with pool.Fori(1, NB):
                pool.wait_ge(ut_used, 1)
                spend(pool, ut_used)
                nc.gpsimd.memset(UT[:], 0.0).then_inc(sums_done, 1)

        @block.scalar
        def _(act):
            for b in range(RING):
                act.sem_inc(hi_free[b], 1)
            act.sem_inc(st_free[0], 1)

            def prepare(k, J, quarters=range(NQ)):
                for q in quarters:
                    operand(k, J, q)
                    split_hi((q + 1) % NQ)

            def split_hi(q):
                act.wait_ge(raw_ready[q], 16)
                spend(act, raw_ready[q], 16)
                for s in range(SUB):
                    b = (q * SUB + s) % RING
                    act.wait_ge(hi_free[b], 1)
                    spend(act, hi_free[b])
                    nc.scalar.copy(hi[:, b], raw[:, q, s]).then_inc(hi_ready[b], 1)

            def operand(k, J, q):
                b = q % 2
                act.wait_ge(st_free[b], 1)
                spend(act, st_free[b])
                g = bass.ds(J * Q + q * SUB, SUB)
                if k == 5:
                    src, dst = T[:, :, g, ph(0)], st[:, b, :, :, ph(0)]
                else:
                    src, dst = T[:, :, g, :], st[:, b]
                nc.scalar.copy(dst, src.bitcast(f32)).then_inc(st_ready[b], 1)

            def hidden(k, I, c):
                if k == 1:
                    act.wait_ge(h_ready, 1)
                    spend(act, h_ready)
                    nc.scalar.activation(hT[:, c, :], PST, ACT.Tanh, bias=hb_sb[:, 0, c:c + 1]).then_inc(
                        tanh_ready, 1)
                    if c == 0:
                        nc.scalar.copy(TT[:], SV[0:D, bass.ds(I * BLK, BLK)]).then_inc(x_ready, 1)

            def evacuate(k, I):
                u, v = ph(u_slot(k)), ph(1 - u_slot(k))
                cols = bass.ds(I * BLK, BLK)
                if k == 1:
                    act.wait_ge(b_done, 1)
                    spend(act, b_done)
                    nc.scalar.copy(UT[:], PSB).then_inc(b_free, 1)
                    nc.scalar.copy(SV[v, cols], PSA[v, :]).then_inc(evac_done, 1)
                else:
                    act.wait_ge(a_done, 1)
                    spend(act, a_done)
                    nc.scalar.copy(UT[u, :], PSA[u, :]).then_inc(evac_done, 1)
                    if k < 5:
                        nc.scalar.copy(SV[v, cols], PSA[v, :]).then_inc(a_free, 1)

            def transposed(k, stage):
                if (k, stage) in ((5, 0), (5, 2), (1, 2)):
                    act.wait_ge(tp_ready, 1)
                    spend(act, tp_ready)
                    nc.scalar.copy(TT[:], PST[0:D, :]).then_inc(tt_ready, 1)

            def root():
                act.wait_ge(var_ready, 1)
                spend(act, var_ready)
                nc.scalar.activation(st2[:], st1[:], ACT.Sqrt).then_inc(sd_ready, 1)

            def row(k, r, prev, upper, older, newest):
                I = block_of(k, r)
                same = prev and prev[0] == k
                if prev and not same:
                    split_hi(1)
                    evacuate(*prev)
                    transposed(prev[0], 0)
                    hidden(*prev, 0)
                    hidden(*prev, 1)
                    if prev[0] in (1, 4):
                        root()
                    transposed(prev[0], 2)
                    act.wait_ge(v_ready, 1)
                    spend(act, v_ready)
                    operand(k, I, 0)
                    operand(k, I, 1)
                else:
                    prepare(k, I, (0,))
                    if older and k == 5:
                        transposed(k, 2)
                    if same:
                        evacuate(*prev)
                        transposed(k, 0)
                        hidden(*prev, 0)
                    operand(k, I, 1)
                    if same:
                        hidden(*prev, 1)
                        if k == 1:
                            nc.scalar.activation(spare[:], relu_bias[:], ACT.Sqrt, scale=0.0)
                split_hi(2)
                prepare(k, I, (2, 3))
                if same and k in (1, 5):
                    root()
                if upper:
                    above(act, r, lambda J: prepare(k, J))
                if older:
                    older_units(act, k, r, lambda J: prepare(k, J))
                if same and k == 4:
                    root()
                if same and k < 5:
                    act.wait_ge(v_ready, 1)
                    spend(act, v_ready)
                if newest:
                    new = block_of(k, r - 1)
                    if k == 5 and older:
                        root()
                    prepare(k, new, (0,))
                    operand(k, new, 1)
                    if k == 5 and not older:
                        root()
                    split_hi(2)
                    prepare(k, new, (2, 3))
                if same and k < 5:
                    transposed(k, 2)

            act.wait_ge(pool_const, 1)
            act.wait_ge(t_start, 1)
            split_hi(0)
            for k in range(1, 6):
                sweep_rows(act, k, row)
            transposed(5, 2)
            evacuate(5, block_of(5, NB - 1))
            transposed(5, 0)
            root()
            root()
            transposed(5, 2)
            act.sem_inc(raw_ready[0], 16)

            for b in range(2):
                act.sem_inc(w_free[b], 1)

            def weights(first=range(Q)):
                for n in first:
                    b = n % 2
                    act.wait_ge(r_ready[b], 1)
                    spend(act, r_ready[b])
                    act.wait_ge(w_free[b], 1)
                    spend(act, w_free[b])
                    nc.scalar.activation(Wt[:, b, :], (PSF_flat, PST)[b], ACT.Relu, scale=-128.0,
                                         bias=relu_bias[:, 0:1]).then_inc(w_ready[b], 1)

            def store(I):
                act.wait_ge(out_ready, 1)
                spend(act, out_ready)
                act.dma_start(out[bass.ds(I, 1)].rearrange("o p q d -> (o p) q d"), xr[:]).then_inc(out_all, 16)

            weights()
            with act.Fori(1, NB):
                weights()
            with act.Fori(1, NB) as I:
                weights()
                weights(range(0, 4))
                root()
                weights(range(4, Q))
                store(I - 1)
                with act.Fori(2, NB):
                    weights()
            root()
            store(NB - 1)
            act.wait_ge(out_all, 16)

        @block.vector
        def _(dve):
            def link(ins):
                ins.then_inc(dve_chain, 1)
                dve.wait_ge(dve_chain, 1)
                spend(dve, dve_chain)

            def rows(col):
                return col.unsqueeze(2).broadcast_to([P, Q, D])

            def feats(row):
                return row.unsqueeze(1).broadcast_to([P, Q, D])

            for b in range(RING):
                dve.sem_inc(lo_free[b], 1)
            tt, ts = nc.vector.tensor_tensor, nc.vector.tensor_scalar
            stt, copy = nc.vector.scalar_tensor_tensor, nc.vector.tensor_copy

            dve.wait_ge(c_x, 32)
            link(copy(T[:, 0, :, ph(0)], O[:]))
            link(tt(T[:, 1, :, ph(0)], O[:], T[:, 0, :, ph(0)].bitcast(f32), ALU.subtract))
            dve.wait_ge(c_hid, 48)
            tt(O[:], O[:], bias[:, 0, :].unsqueeze(1).broadcast_to([P, G, D]), ALU.add)
            link(tt(hb_sb[:, 0, :], hb_sb[:, 0, :], hb_sb[:, 2, :], ALU.mult))
            tt(hb_sb[:, 0, :], hb_sb[:, 0, :], hb_sb[:, 1, :], ALU.add).then_inc(t_start, 1)
            dve.wait_ge(c_rest, 64)
            dve.wait_ge(c_hid2, 96)
            dve.wait_ge(pool_const, 1)
            a0, a1 = ph(0), ph(1)
            copy(rank_b[:], rank_f[:])
            copy(pick1[a0, 0:D], bt_sb[:])
            tt(w02[:], l1w_sb[a0, 0, :], l1w_sb[a0, 2, :], ALU.subtract)
            copy(comb[a1, 0:D], eye[a1, D:2 * D])
            tt(comb[a1, D:2 * D], l1w_sb[a1, 1, :], l1w_sb[a1, 3, :], ALU.subtract)
            ts(comb[a0, 0:D], eye[a0, 0:D], 2.0, None, ALU.mult)
            ts(comb[a0, D:2 * D], l1w_sb[a0, 2, :], 2.0, None, ALU.mult)
            nc.vector.memset(relu_bias[:], float(128 * (CUT - MARK)))
            ts(comb4[a1, :], l1w_sb[a1, 3, :], 2.0, None, ALU.mult).then_inc(const_ready, 1)

            def split_lo(quarters, sums=False):
                for q in quarters:
                    for s in range(SUB):
                        b = (q * SUB + s) % RING
                        dve.wait_ge(hi_ready[b], 1)
                        spend(dve, hi_ready[b])
                        dve.wait_ge(lo_free[b], 1)
                        spend(dve, lo_free[b])
                        tt(lo[:, b], raw[:, q, s], hi[:, b].bitcast(f32), ALU.subtract).then_inc(
                            lo_ready[b] if s else lo_done, 1)
                    dve.wait_ge(lo_done, 1)
                    spend(dve, lo_done)
                    dve.sem_inc(lo_ready[q * SUB % RING], 1)
                    dve.sem_inc(raw_free[(q - 1) % NQ], 1)
                    if sums:
                        dve.wait_ge(sums_done, 1)
                        spend(dve, sums_done)
                        tt(UT[:], UT[:], raw[:, q, SUB - 1], ALU.add).then_inc(sums_done, 1)

            def add_partial(k, I):
                u = ph(u_slot(k))
                dve.wait_ge(evac_done, 1)
                spend(dve, evac_done)
                if k == 1:
                    tt(UT[u, :], UT[u, :], PSA[u, :], ALU.add).then_inc(ut_ready, 1)
                else:
                    tt(UT[u, :], UT[u, :], SV[u, bass.ds(I * BLK, BLK)], ALU.add).then_inc(ut_ready, 1)

            def add_diagonal(k, I):
                if k > 1:
                    u, cols = ph(u_slot(k)), bass.ds(I * BLK, BLK)
                    dve.wait_ge(b_done, 1)
                    spend(dve, b_done)
                    link(tt(SV[u, cols], SV[u, cols], PSB[u, :], ALU.add))
                    dve.sem_inc(b_free, 1)

            def row_sums():
                link(nc.vector.tensor_reduce(st1[:], xr[:], AX, ALU.add))

            def less_means():
                link(stt(xr[:], rows(st1[:]), -1.0 / D, xr[:], ALU.mult, ALU.add))

            def squares():
                link(tt(sq[:], xr[:], xr[:], ALU.mult))

            def variances():
                link(nc.vector.tensor_reduce(st1[:], sq[:], AX, ALU.add))
                ts(st1[:], st1[:], 1.0 / D, EPS, ALU.mult, ALU.add).then_inc(var_ready, 1)

            def centre():
                row_sums()
                less_means()
                squares()
                variances()

            def scale():
                dve.wait_ge(sd_ready, 1)
                spend(dve, sd_ready)
                link(nc.vector.reciprocal(st3[:], st2[:]))
                return tt(xr[:], xr[:], rows(st3[:]), ALU.mult)

            def whole(k, I):
                if k in (3, 5):
                    src = T[:, :, bass.ds(I * Q, Q), ph(1 if k == 3 else 0)].bitcast(f32)
                    ins = tt(xo[:], src[:, 0], src[:, 1], ALU.add)
                    if k == 5:
                        ins.then_inc(xo_ready, 1)
                    else:
                        link(ins)

            def write_v(k, I):
                dst = T[:, :, bass.ds(I * Q, Q), ph(1 - u_slot(k))]
                link(copy(dst[:, 0], xr[:]))
                tt(dst[:, 1], xr[:], dst[:, 0].bitcast(f32), ALU.subtract).then_inc(v_ready, 1)

            def finish_first(k, I):
                g = bass.ds(I * Q, Q)
                f0, f1 = PSF[:, :, 0:D], PSF[:, :, D:2 * D]
                dve.wait_ge(fin_ready, 1)
                spend(dve, fin_ready)
                if k == 1:
                    dve.sem_inc(ut_used, 1)
                    link(copy(RS[:, g], PSF[:, :, D]))
                    link(tt(sq[:], PST[:, 0:Q * D].rearrange("p (q d) -> p q d", q=Q), rows(RS[:, g]), ALU.mult))
                    link(tt(xr[:], f0, sq[:], ALU.subtract))
                    tt(xr[:], xr[:], O[:, g, :], ALU.add).then_inc(dve_chain, 1)
                    dve.wait_ge(dve_chain, 1)
                    spend(dve, dve_chain)
                elif k == 2:
                    link(copy(xr[:], f0))
                elif k == 3:
                    link(tt(xr[:], f0, xo[:], ALU.subtract))
                elif k == 4:
                    link(tt(xr[:], f0, O[:, g, :], ALU.add))
                else:
                    link(tt(sq[:], f1, rows(RD[:, g]), ALU.mult))
                    link(tt(xr[:], f0, sq[:], ALU.add))
                    link(tt(xr[:], xr[:], feats(bias[:, 2, :]), ALU.add))
                    link(stt(sq[:], xr[:], 0.0, xr[:], ALU.max, ALU.mult))
                    nc.vector.tensor_reduce(st1[:], sq[:], AX, ALU.add).then_inc(var_ready, 1)

            def finish_middle(k):
                if k in (1, 4):
                    centre()

            def finish_last(k, I):
                if k == 1:
                    link(scale())
                    dve.sem_inc(xr_pe, 1)
                    write_v(k, I)
                elif k in (2, 3):
                    write_v(k, I)
                elif k == 4:
                    link(scale())
                    write_v(k, I)
                elif k == 5:
                    dve.wait_ge(sd_ready, 1)
                    spend(dve, sd_ready)
                    link(ts(st3[:], st2[:], L2_EPS, None, ALU.max))
                    link(nc.vector.reciprocal(st3[:], st3[:]))
                    link(stt(xr[:], xr[:], 0.0, rows(st3[:]), ALU.max, ALU.mult))
                    link(tt(xr[:], xr[:], xo[:], ALU.add))

            def outputs(k, I):
                if k in (2, 3):
                    g = bass.ds(I * Q, Q)
                    link(tt(O[:, g, :], O[:, g, :], PSF[:, :, D:2 * D], ALU.add))

            def norm_first(k):
                if k == 5:
                    centre()

            def norm_last(k, I):
                if k == 5:
                    link(scale())
                    copy(O[:, bass.ds(I * Q, Q), :], xr[:]).then_inc(xr_pe, 1)

            def support():
                dve.wait_ge(fin2_ready, 1)
                spend(dve, fin2_ready)
                link(ts(sq[:], PSF[:, :, 0:D], SCALE, None, ALU.mult))

            def support_parts(I, parts=(0, 1)):
                g = bass.ds(I * Q, Q)
                s1, s2, s3 = S[:, g, 0:D], S[:, g, D:2 * D], S[:, g, 2 * D:3 * D]
                if 0 in parts:
                    link(copy(s1, sq[:]))
                    link(tt(sq[:], sq[:], s1, ALU.subtract))
                if 1 in parts:
                    link(copy(s2, sq[:]))
                    link(tt(s3, sq[:], s2, ALU.subtract))

            def after(k, I):
                g = bass.ds(I * Q, Q)
                if k == 1:
                    link(ts(RD[:, g], RS[:, g], 1.0, 1.0, ALU.add, ALU.max))
                    nc.vector.reciprocal(RD[:, g], RD[:, g])
                    dve.wait_ge(fin2_ready, 1)
                    spend(dve, fin2_ready)
                    link(tt(O[:, g, :], xr[:], PSF[:, :, 0:D], ALU.add))
                    link(tt(O[:, g, :], O[:, g, :], feats(bias[:, 1, :]), ALU.add))
                elif k == 5:
                    support()
                    support_parts(I)

            def row(k, r, prev, upper, older, newest):
                same = prev and prev[0] == k
                late = k == 5 and older
                if prev and prev[0] == 3:
                    whole(*prev)
                split_lo((0, 1))
                if prev:
                    add_partial(*prev)
                if late:
                    support()
                    dve.sem_inc(psf_free, 1)
                    support_parts(r - 2, (0,))
                if prev and not same:
                    finish_first(*prev)
                    finish_middle(prev[0])
                    finish_last(*prev)
                    outputs(*prev)
                    after(*prev)
                split_lo((2,))
                if late:
                    support_parts(r - 2, (1,))
                split_lo((3,))
                sums = k == 1
                spread = k in (4, 5) and older
                if same:
                    finish_first(*prev)
                    if not spread:
                        finish_middle(k)
                if upper:
                    above(dve, r, lambda J: split_lo(range(NQ)))
                if same and k == 1:
                    finish_last(*prev)
                if spread:
                    if not isinstance(r, int):
                        with dve.Fori(0, r - 2):
                            split_lo(range(NQ))
                    split_lo((0,))
                    if k == 5:
                        finish_last(*prev)
                    split_lo((1,))
                    row_sums()
                    less_means()
                    split_lo((2,))
                    squares()
                    variances()
                    split_lo((3,))
                elif older:
                    older_units(dve, k, r, lambda J: split_lo(range(NQ), sums))
                if same and k > 1 and not (spread and k == 5):
                    finish_last(*prev)
                if newest:
                    split_lo((0,), sums)
                    outputs(*prev)
                    if spread:
                        norm_last(*prev)
                    else:
                        norm_first(k)
                    split_lo((1,), sums)
                    if k == 5:
                        if not spread:
                            norm_last(*prev)
                        whole(k, block_of(k, r))
                    split_lo((2,), sums)
                    add_diagonal(k, block_of(k, r))
                    split_lo((3,), sums)
                if newest and sums:
                    dve.wait_ge(sums_done, 1)
                    spend(dve, sums_done)
                    dve.sem_inc(sums_ready, 1)
                if same and k < 5:
                    after(*prev)
                if not newest:
                    if k == 5:
                        whole(k, block_of(k, r))
                    add_diagonal(k, block_of(k, r))

            for k in range(1, 6):
                sweep_rows(dve, k, row, peeled=3 if k > 3 else 2)
            last = block_of(5, NB - 1)
            support()
            dve.sem_inc(raw_free[NQ - 1], 1)
            support_parts(last - 1)
            add_partial(5, last)
            finish_first(5, last)
            finish_last(5, last)
            norm_first(5)
            norm_last(5, last)
            after(5, last)

            dve.sem_inc(s_ready, 1)
            for b in range(SUB):
                dve.wait_ge(hi_ready[b], 1)
                spend(dve, hi_ready[b])
            dve.sem_inc(half_done[0], 1)
            for n in range(1, Q - 1):
                dve.sem_inc(m_free[n], 1)
            dve.sem_inc(out_all, 16)

            def count(n, first=False, behind=True):
                k = n // SUB
                if n % SUB == 0:
                    dve.wait_ge(raw_ready[k], 16)
                    spend(dve, raw_ready[k], 16)
                dve.wait_ge(m_free[(n + 1) % Q], 1)
                spend(dve, m_free[(n + 1) % Q])
                for h in range(2):
                    cols = slice(h * HALF, (h + 1) * HALF)
                    src = raw[:, k, SUB - 1 - n % SUB, cols]
                    old, new = M[:, n, cols], M[:, (n + 1) % Q, cols]
                    if h == 0:
                        dve.wait_ge(half_done[0], 1)
                        spend(dve, half_done[0])
                    elif behind:
                        counted((n - 1) % Q)
                    if first and n == 0:
                        ins = ts(new, src, 0.0, None, ALU.not_equal)
                    else:
                        ins = stt(new, src, 0.0, old, ALU.not_equal, ALU.add)
                    ins.then_inc(half_done[h], 1)

            def counted(n):
                dve.wait_ge(half_done[1], 1)
                spend(dve, half_done[1])
                dve.sem_inc(m_ready[n], 1)
                if n % SUB == SUB - 1:
                    dve.sem_inc(raw_free[n // SUB], 1)

            def gather():
                dve.wait_ge(o_done, 1)
                spend(dve, o_done)
                dve.wait_ge(out_all, 16)
                spend(dve, out_all, 16)
                link(nc.vector.tensor_reduce(
                    xr[:].rearrange("p (a b) d -> p a b d", b=2),
                    PSAB[:, :, 0:6 * D].rearrange("p a (b t d) -> p a b d t", b=2, t=3), AX, ALU.add))
                dve.sem_inc(o_free, 1)

            def add_bias():
                link(tt(xr[:], xr[:], feats(bias[:, 3, :]), ALU.add))

            def add_residual(I):
                link(tt(xr[:], xr[:], O[:, bass.ds(I * Q, Q), :], ALU.add))

            def counts(I, prev):
                for n in range(Q):
                    count(n, first=True, behind=prev is not None or n > 0)
                    if prev is not None and n == 5:
                        gather()
                    if prev is not None and n == 6:
                        add_bias()
                    if prev is not None and n == 7:
                        add_residual(prev)
                for n in range(Q if prev is not None else 0):
                    count(n)
                    if n == 0:
                        row_sums()
                    if n == 1:
                        less_means()
                    if n == 2:
                        squares()
                    if n == 3:
                        variances()
                if prev is not None:
                    scale().then_inc(out_ready, 1)
                with dve.Fori(1 if prev is None else 2, NB):
                    for n in range(Q):
                        count(n)

            counts(0, None)
            with dve.Fori(1, NB) as I:
                counts(I, I - 1)
            counted(Q - 1)
            gather()
            add_bias()
            add_residual(NB - 1)
            centre()
            scale().then_inc(out_ready, 1)

        @block.tensor
        def _(pe):
            mm = nc.tensor.matmul

            def small(dst, lhs, rhs, **kw):
                for q in range(Q):
                    last = mm(dst[:, q, :], lhs[:, q * P:(q + 1) * P], rhs, start=True, stop=True)
                return last

            pe.sem_inc(b_free, 1)
            pe.sem_inc(a_free, 1)
            pe.wait_ge(pool_const, 1)
            pe.wait_ge(const_ready, 1)

            def multiply(bank, quarters=range(NQ), sums_bank=None, start=False, stop=False):
                for q in quarters:
                    pe.wait_ge(st_ready[q % 2], 1)
                    spend(pe, st_ready[q % 2])
                    for s in range(SUB):
                        b = (q * SUB + s) % RING
                        first, last = start and q + s == 0, stop and q == NQ - 1 and s == SUB - 1
                        w_hi, w_lo = st[:, q % 2, 0, s, :], st[:, q % 2, 1, s, :]
                        pe.wait_ge(lo_ready[b], 1)
                        spend(pe, lo_ready[b])
                        rows_too = sums_bank is not None and s < SUB - 1
                        terms = [(bank, w_hi, lo)] + [(sums_bank, ones_st[:], lo)] * rows_too
                        n_lo = 2 * len(terms)
                        terms += [(bank, w_hi, hi), (bank, w_lo, hi)]
                        terms += [(sums_bank, ones_st[:], hi)] * rows_too
                        for n in range(2 * len(terms)):
                            dst, w, src = terms[n // 2]
                            cols = slice(n % 2 * HALF, (n % 2 + 1) * HALF)
                            ins = mm(dst[:, cols], w, src[:, b, cols], start=first and n < 2,
                                     stop=last and n >= 2 * len(terms) - 2)
                            if n == 0 and s == 0:
                                ins.then_inc(st_free[(q - 1) % 2], 1)
                            elif n == n_lo - 1:
                                ins.then_inc(lo_free[b], 1)
                            elif n == 2 * len(terms) - 1:
                                ins.then_inc(hi_free[b], 1)

            def zeros(bank, start):
                for h in range(2):
                    last = mm(bank[:, h * HALF:(h + 1) * HALF], zst[:], zmv[:], start=start, stop=not start)
                return last

            def transpose(src):
                for q in range(Q):
                    last = mm(PST[0:D, q * P:(q + 1) * P], src[:, q, :], eye[:], start=True, stop=True)
                last.then_inc(tp_ready, 1)

            def hidden(k, I, c):
                if k == 1:
                    if c > 0:
                        pe.wait_ge(tanh_ready, 1)
                        spend(pe, tanh_ready)
                    for h in range(2):
                        last = mm(PST[:, h * HALF:(h + 1) * HALF], w1_sb[:, c * P:(c + 1) * P],
                                  SV[0:D, bass.ds(I * BLK + h * HALF, HALF)], start=True, stop=True)
                    last.then_inc(h_ready, 1)

            def end0(k, I):
                if k == 5:
                    pe.wait_ge(xo_ready, 1)
                    spend(pe, xo_ready)
                    transpose(xo)

            def end1(k, I):
                u = ph(u_slot(k))
                if k == 1:
                    pe.wait_ge(tanh_ready, 1)
                    spend(pe, tanh_ready)
                    pe.wait_ge(x_ready, 1)
                    spend(pe, x_ready)
                    for q in range(Q):
                        mm(PST[:, q * D:(q + 1) * D], TT[:, q * P:(q + 1) * P], bt_sb[:], start=True, stop=True)
                pe.wait_ge(ut_ready, 1)
                spend(pe, ut_ready)
                if k == 1:
                    for q in range(Q):
                        cols = slice(q * P, (q + 1) * P)
                        mm(PSF[:, q, 0:D + 1], UT[:, cols], pick1[:], start=True, stop=False)
                        for c in range(HC):
                            last = mm(PSF[:, q, 0:D], hT[:, c, cols], w2_sb[:, c, :], start=False, stop=c == HC - 1)
                elif k < 4:
                    last = small(PSF, UT[u, :], comb[u, :])
                elif k == 4:
                    last = small(PSF[:, :, 0:D], UT[u, :], comb4[u, :])
                else:
                    pe.wait_ge(tt_ready, 1)
                    spend(pe, tt_ready)
                    for q in range(Q):
                        mm(PSF[:, q, :], TT[:, q * P:(q + 1) * P], l2w_sb[:], start=True, stop=False)
                        last = mm(PSF[:, q, D:2 * D], UT[u, q * P:(q + 1) * P], l2w_sb[:, D:2 * D],
                                  start=False, stop=True)
                last.then_inc(fin_ready, 1)

            def end2(k, I):
                if k in (1, 5):
                    pe.wait_ge(xr_pe, 1)
                    spend(pe, xr_pe)
                    transpose(xr)

            def end3(k, I):
                if k in (1, 5):
                    pe.wait_ge(tt_ready, 1)
                    spend(pe, tt_ready)
                    small(PSF[:, :, 0:D], TT, w02[:] if k == 1 else l3w_sb[:]).then_inc(fin2_ready, 1)

            def row(k, r, prev, upper, older, newest):
                same = prev and prev[0] == k
                sums = PSB if k == 1 else None
                if prev:
                    hidden(*prev, 0)
                if prev and not same:
                    hidden(*prev, 1)
                    end1(*prev)
                    end2(*prev)
                    end3(*prev)
                pe.wait_ge(b_free, 1)
                spend(pe, b_free)
                multiply(PSB, (0,), start=True)
                if k == 5 and older:
                    end3(*prev)
                if same:
                    end0(*prev)
                    hidden(*prev, 1)
                multiply(PSB, (1,))
                if k == 5 and older:
                    pe.wait_ge(psf_free, 1)
                    spend(pe, psf_free)
                if same:
                    end1(*prev)
                multiply(PSB, (2, 3), stop=k > 1)
                if k > 1:
                    mm(PST[:, 0:2], zst[:], zmv[:, 0:2], start=True, stop=True).then_inc(b_done, 1)
                if upper:
                    above(pe, r, lambda J: multiply(PSB))
                if 2 <= k <= 4 or (k == 5 and not same):
                    pe.wait_ge(a_free, 1)
                    spend(pe, a_free)
                zeros(PSA, True)
                if older:
                    older_units(pe, k, r, lambda J: multiply(PSA, sums_bank=sums))
                if newest:
                    multiply(PSA, (0, 1), sums_bank=sums)
                    if k == 1:
                        end2(*prev)
                    multiply(PSA, (2, 3), sums_bank=sums)
                if same:
                    if k == 5:
                        end2(*prev)
                    else:
                        end3(*prev)
                last = zeros(PSA, False)
                if k == 1:
                    if newest:
                        pe.wait_ge(sums_ready, 1)
                        spend(pe, sums_ready)
                        for h in range(2):
                            last = mm(PSB[:, h * HALF:(h + 1) * HALF], ones_st[:].bitcast(f32),
                                      UT[:, h * HALF:(h + 1) * HALF], start=False, stop=True)
                    else:
                        last = zeros(PSB, False)
                    last.then_inc(b_done, 1)
                else:
                    last.then_inc(a_done, 1)

            for k in range(1, 6):
                sweep_rows(pe, k, row)
            last = block_of(5, NB - 1)
            end3(5, last - 1)
            end0(5, last)
            end1(5, last)
            end2(5, last)
            end3(5, last)

            pe.wait_ge(s_ready, 1)
            spend(pe, s_ready)
            pe.sem_inc(o_free, 1)
            ranks = (PSF_flat, PST)

            def rank(n, first=False):
                b, old, new = n % 2, n, (n + 1) % Q
                pe.wait_ge(m_ready[n], 1)
                spend(pe, m_ready[n])
                terms = [(0, new, h) for h in range(2)] + [(1, old, h) for h in range(2)] * (not first)
                for i, (m, src, h) in enumerate(terms):
                    ins = mm(ranks[b][:, h * HALF:(h + 1) * HALF], rank_b[:, m, :],
                             M[:, src, h * HALF:(h + 1) * HALF], start=i < 2, stop=i >= len(terms) - 2)
                    if i == 0:
                        ins.then_inc(m_free[(n - 1) % Q], 1)
                    elif i == len(terms) - 1:
                        ins.then_inc(r_ready[b], 1)

            def weigh(n, J):
                b = n % 2
                pe.wait_ge(w_ready[b], 1)
                spend(pe, w_ready[b])
                g = J * Q + (Q - 1 - n)
                for q in range(Q):
                    last = mm(PSAB[:, q // 2, (q % 2) * 3 * D:(q % 2 + 1) * 3 * D],
                              Wt[:, b, q * P:(q + 1) * P].bitcast(bf16), S[:, bass.ds(g, 1), :].rearrange(
                                  "p o n -> p (o n)"), start=False, stop=False)
                last.then_inc(w_free[b], 1)

            def bounds(start):
                for a in range(4):
                    last = mm(PSAB[:, a, 0:6 * D], zst[:], zmv[:, 0:6 * D], start=start, stop=not start)
                return last

            def weighted_row(first_row):
                rank(0, first=True)
                if not first_row:
                    weigh(Q - 1, 0)
                    bounds(False).then_inc(o_done, 1)
                rank(1)
                pe.wait_ge(w_ready[0], 1)
                rank(2)
                pe.wait_ge(o_free, 1)
                spend(pe, o_free)
                bounds(True)
                weigh(0, NB - 1)
                weigh(1, NB - 1)
                for n in range(3, Q):
                    rank(n)
                    weigh(n - 1, NB - 1)
                with pe.Fori(1, NB) as o:
                    rank(0)
                    weigh(Q - 1, NB - o)
                    for n in range(1, Q):
                        rank(n)
                        weigh(n - 1, NB - 1 - o)

            weighted_row(first_row=True)
            with pe.Fori(1, NB):
                weighted_row(first_row=False)
            weigh(Q - 1, 0)
            bounds(False).then_inc(o_done, 1)


_INS = ["at", "x_rows", "x_cols", "t_col", "b_t", "w1", "w1_t", "b1_c", "w2", "bias_rows", "l1_w", "l2_w",
        "l3_w", "ident", "rank_mats"]


def lay_out(x, adj, L0_gnn_t, L0_gnn_B, L0_gnn_W1, L0_gnn_b1, L0_gnn_W2, L0_gnn_b2, L1_gnn_weights,
            L1_gnn_bias, L2_gnn_W, L2_gnn_b, L3_gnn_weight, L3_gnn_bias):
    import numpy as np
    P, BLK = 128, 1024
    c = np.ascontiguousarray
    x, adj = np.asarray(x), np.asarray(adj)
    N, D = x.shape
    NB, Q = N // BLK, BLK // P
    w1 = np.asarray(L0_gnn_W1)
    HID = w1.shape[1]
    later = np.tril(np.ones((P, P), np.float32), -1) - 127 * np.eye(P, dtype=np.float32)
    return {
        "at": c(adj.reshape(NB, BLK, NB, 4, Q // 4, P).transpose(0, 2, 3, 5, 4, 1)).reshape(
            NB * NB * 4, P, (Q // 4) * BLK),
        "x_rows": c(x.reshape(N // P, P, D).transpose(1, 0, 2)),
        "x_cols": c(x.T),
        "t_col": c(np.broadcast_to(np.asarray(L0_gnn_t).reshape(1, 1), (P, HID // P))),
        "b_t": c(np.asarray(L0_gnn_B).T),
        "w1": c(w1[:D]),
        "w1_t": c(w1[D].reshape(HID // P, P).T),
        "b1_c": c(np.asarray(L0_gnn_b1).reshape(HID // P, P).T),
        "w2": c(np.asarray(L0_gnn_W2).reshape(HID // P, P, D).transpose(1, 0, 2)),
        "bias_rows": c(np.broadcast_to(np.stack([np.asarray(b) for b in (
            L0_gnn_b2, L1_gnn_bias, L2_gnn_b, L3_gnn_bias)])[None], (P, 4, D))),
        "l1_w": c(np.asarray(L1_gnn_weights).transpose(1, 0, 2)),
        "l2_w": c(np.asarray(L2_gnn_W).reshape(2, D, D).transpose(1, 0, 2)).reshape(D, 2 * D),
        "l3_w": c(np.asarray(L3_gnn_weight)),
        "ident": np.eye(P, dtype=np.float32),
        "rank_mats": c(np.stack([later, 1 - later], 1)),
    }


def build(nc, arrays, N, D):
    args = [nc.dram_tensor(f"in_{n}", arrays[n].shape, mybir.dt.float32, kind="ExternalInput").ap() for n in _INS]
    out = nc.dram_tensor("out_0", (N // 1024, 128, 8, D), mybir.dt.float32, kind="ExternalOutput").ap()
    graph_layers(nc, *args, out)


def kernel(**inputs):
    import numpy as np
    import concourse.bacc as bacc
    from concourse.bass_utils import run_bass_kernel_spmd

    arrays = lay_out(**inputs)
    N, D = inputs["x"].shape
    nc = bacc.Bacc("TRN2", target_bir_lowering=False, num_devices=1)
    build(nc, arrays, N, D)
    r = run_bass_kernel_spmd(nc, [{f"in_{n}": a for n, a in arrays.items()}], core_ids=[0])
    return np.ascontiguousarray(np.asarray(r.results[0]["out_0"]).transpose(0, 2, 1, 3)).reshape(N, D)
```
